# Optimizing a Trainium2 kernel written in Bass

```python
import numpy as np
import jax
import jax.numpy as jnp

def _softmax(x, axis=-1):
    return jax.nn.softmax(x, axis=axis)

def _gelu(x):
    return jax.nn.gelu(x, approximate=True)

def _silu(x):
    return jax.nn.silu(x)

def _sigmoid(x):
    return jax.nn.sigmoid(x)

def _layernorm(x, axis=-1, eps=1e-05):
    m = jnp.mean(x, axis=axis, keepdims=True)
    v = jnp.var(x, axis=axis, keepdims=True)
    return (x - m) / jnp.sqrt(v + eps)

def _scatter_add(tgt, idx, src, axis=0):
    return tgt.at[idx].add(src)

def _segment_sum(src, seg, n):
    return jax.ops.segment_sum(src, seg, n)
kernel_name = 'mk_sandwich_d1_jaxref_r8_a5c188'

def setup_inputs(seed: int=0):
    np.random.seed(seed)
    _w = jnp.asarray

    def _L0_attn_setup():
        import jax, jax.numpy as jnp
        import numpy as np
        D_MODEL = 128
        N_HEADS = 16
        HEAD_DIM = D_MODEL // N_HEADS
        WINDOW = 128
        ROPE_BASE = 10000.0

        def _rope_cos_sin(T, dim, dtype):
            inv_freq = 1.0 / ROPE_BASE ** (jnp.arange(0, dim, 2, dtype=jnp.float32) / dim)
            freqs = jnp.arange(T, dtype=jnp.float32)[:, None] * inv_freq[None, :]
            emb = jnp.concatenate([freqs, freqs], axis=-1)
            return (jnp.cos(emb).astype(dtype), jnp.sin(emb).astype(dtype))

        def _rotate_half(x):
            h = x.shape[-1] // 2
            return jnp.concatenate([-x[..., h:], x[..., :h]], axis=-1)

        def _apply_rotary(x, cos, sin):
            c = cos[None, :, None, :]
            s = sin[None, :, None, :]
            return x * c + _rotate_half(x) * s
        key = jax.random.key(seed)
        ks = jax.random.split(key, 6)
        B, T = (2, 256)
        query = jax.random.normal(ks[0], (B, T, D_MODEL), dtype=jnp.float32)
        scale = 1.0 / np.sqrt(D_MODEL)
        Wq = jax.random.normal(ks[1], (D_MODEL, D_MODEL), dtype=jnp.float32) * scale
        Wk = jax.random.normal(ks[2], (D_MODEL, D_MODEL), dtype=jnp.float32) * scale
        Wv = jax.random.normal(ks[3], (D_MODEL, D_MODEL), dtype=jnp.float32) * scale
        Wo = jax.random.normal(ks[4], (D_MODEL, D_MODEL), dtype=jnp.float32) * scale
        bo = jax.random.normal(ks[5], (D_MODEL,), dtype=jnp.float32) * 0.01
        return {'query': query, 'Wq': Wq, 'Wk': Wk, 'Wv': Wv, 'Wo': Wo, 'bo': bo}
    _L0_attn_in = _L0_attn_setup()

    def _L0_ffn_setup():
        import jax, jax.numpy as jnp
        import numpy as np
        E = 8
        C = 160
        D = 128
        H = 512
        B, S = (4, 256)
        key = jax.random.key(seed)
        ks = jax.random.split(key, 12)
        sc = 0.02
        return {'input': jax.random.normal(ks[0], (B, S, D), jnp.float32), 'router_w': jax.random.normal(ks[1], (D, E), jnp.float32) * sc, 'router_b': jnp.zeros((E,), jnp.float32), 'w1': jax.random.normal(ks[2], (E, D, H), jnp.float32) * sc, 'b1': jnp.zeros((E, H), jnp.float32), 'w2': jax.random.normal(ks[3], (E, H, D), jnp.float32) * sc, 'b2': jnp.zeros((E, D), jnp.float32), 'ow1': jax.random.normal(ks[4], (D, H), jnp.float32) * sc, 'ob1': jnp.zeros((H,), jnp.float32), 'ow2': jax.random.normal(ks[5], (H, D), jnp.float32) * sc, 'ob2': jnp.zeros((D,), jnp.float32)}
    _L0_ffn_in = _L0_ffn_setup()
    _d = {'L0_attn_query': _L0_attn_in['query'], 'L0_attn_Wq': _L0_attn_in['Wq'], 'L0_attn_Wk': _L0_attn_in['Wk'], 'L0_attn_Wv': _L0_attn_in['Wv'], 'L0_attn_Wo': _L0_attn_in['Wo'], 'L0_attn_bo': _L0_attn_in['bo'], 'L0_ffn_router_w': _L0_ffn_in['router_w'], 'L0_ffn_router_b': _L0_ffn_in['router_b'], 'L0_ffn_w1': _L0_ffn_in['w1'], 'L0_ffn_b1': _L0_ffn_in['b1'], 'L0_ffn_w2': _L0_ffn_in['w2'], 'L0_ffn_b2': _L0_ffn_in['b2'], 'L0_ffn_ow1': _L0_ffn_in['ow1'], 'L0_ffn_ob1': _L0_ffn_in['ob1'], 'L0_ffn_ow2': _L0_ffn_in['ow2'], 'L0_ffn_ob2': _L0_ffn_in['ob2']}
    _x0 = _d['L0_attn_query']
    _d['L0_attn_query'] = jax.random.normal(jax.random.fold_in(jax.random.key(seed), 1), (32, 256, 128), dtype=_x0.dtype)
    del _x0
    return _d

def reference(L0_attn_query, L0_attn_Wq, L0_attn_Wk, L0_attn_Wv, L0_attn_Wo, L0_attn_bo, L0_ffn_router_w, L0_ffn_router_b, L0_ffn_w1, L0_ffn_b1, L0_ffn_w2, L0_ffn_b2, L0_ffn_ow1, L0_ffn_ob1, L0_ffn_ow2, L0_ffn_ob2):

    def _L0_attn_ref(query, Wq, Wk, Wv, Wo, bo):
        import jax, jax.numpy as jnp
        import numpy as np
        D_MODEL = 128
        N_HEADS = 16
        HEAD_DIM = D_MODEL // N_HEADS
        WINDOW = 128
        ROPE_BASE = 10000.0

        def _rope_cos_sin(T, dim, dtype):
            inv_freq = 1.0 / ROPE_BASE ** (jnp.arange(0, dim, 2, dtype=jnp.float32) / dim)
            freqs = jnp.arange(T, dtype=jnp.float32)[:, None] * inv_freq[None, :]
            emb = jnp.concatenate([freqs, freqs], axis=-1)
            return (jnp.cos(emb).astype(dtype), jnp.sin(emb).astype(dtype))

        def _rotate_half(x):
            h = x.shape[-1] // 2
            return jnp.concatenate([-x[..., h:], x[..., :h]], axis=-1)

        def _apply_rotary(x, cos, sin):
            c = cos[None, :, None, :]
            s = sin[None, :, None, :]
            return x * c + _rotate_half(x) * s
        B, T, D = query.shape
        H, Dh = (N_HEADS, HEAD_DIM)
        sm_scale = Dh ** (-0.5)
        q = (query @ Wq.T).reshape(B, T, H, Dh)
        k = (query @ Wk.T).reshape(B, T, H, Dh)
        v = (query @ Wv.T).reshape(B, T, H, Dh)
        cos, sin = _rope_cos_sin(T, Dh, query.dtype)
        q = _apply_rotary(q, cos, sin)
        k = _apply_rotary(k, cos, sin)
        q = q.transpose(0, 2, 1, 3)
        k = k.transpose(0, 2, 1, 3)
        v = v.transpose(0, 2, 1, 3)
        scores = jnp.einsum('bhqd,bhkd->bhqk', q, k) * sm_scale
        i = jnp.arange(T)[:, None]
        j = jnp.arange(T)[None, :]
        mask = (j > i) | (j < i - (WINDOW - 1))
        scores = jnp.where(mask[None, None], jnp.float32(-jnp.inf), scores)
        attn = jax.nn.softmax(scores, axis=-1)
        out = jnp.einsum('bhqk,bhkd->bhqd', attn, v)
        out = out.transpose(0, 2, 1, 3).reshape(B, T, D)
        return out @ Wo.T + bo

    def _L0_ffn_ref(input, router_w, router_b, w1, b1, w2, b2, ow1, ob1, ow2, ob2):
        import jax, jax.numpy as jnp
        import numpy as np
        E = 8
        C = 160
        D = 128
        H = 512
        B, S = (4, 256)
        Bq, Sq, Dq = input.shape
        N = Bq * Sq
        xf = input.reshape(N, Dq)
        probs = jax.nn.softmax(xf @ router_w + router_b, axis=-1)
        eid = jnp.argmax(probs, axis=-1)
        onehot = jax.nn.one_hot(eid, E, dtype=xf.dtype)
        rank = (jnp.cumsum(onehot, axis=0)[jnp.arange(N), eid] - 1.0).astype(jnp.int32)
        valid = rank < C
        pos = jnp.where(valid, rank, 0)
        vmask = valid.astype(xf.dtype)[:, None]
        buf = jnp.zeros((E, C, Dq), xf.dtype).at[eid, pos].add(xf * vmask)
        h = jax.nn.relu(jnp.einsum('ecd,edh->ech', buf, w1) + b1[:, None, :])
        y = jnp.einsum('ech,ehd->ecd', h, w2) + b2[:, None, :]
        y_tok = y[eid, pos] * vmask
        yov = jax.nn.relu(xf @ ow1 + ob1) @ ow2 + ob2
        out = y_tok + yov * (1.0 - vmask)
        return out.reshape(Bq, Sq, Dq)
    x = L0_attn_query
    x = x + _layernorm(_L0_attn_ref(_layernorm(x, axis=-1), L0_attn_Wq, L0_attn_Wk, L0_attn_Wv, L0_attn_Wo, L0_attn_bo), axis=-1)
    x = x + _layernorm(_L0_ffn_ref(_layernorm(x, axis=-1), L0_ffn_router_w, L0_ffn_router_b, L0_ffn_w1, L0_ffn_b1, L0_ffn_w2, L0_ffn_b2, L0_ffn_ow1, L0_ffn_ob1, L0_ffn_ow2, L0_ffn_ob2), axis=-1)
    return x

_drawn_inputs = setup_inputs


def setup_inputs(seed=0):
    import zlib

    import numpy as np

    out = dict(_drawn_inputs(seed))
    spreads = {'L0_ffn_router_b': (0.0, 0.1),
     'L0_ffn_b1': (0.0, 0.1),
     'L0_ffn_b2': (0.0, 0.1),
     'L0_ffn_ob1': (0.0, 0.1),
     'L0_ffn_ob2': (0.0, 0.1)}
    factors = {}
    for name, (base, spread) in spreads.items():
        noise = np.random.default_rng([zlib.crc32(name.encode()), seed]).standard_normal(out[name].shape)
        drawn = base * np.exp(spread * noise) if base else spread * noise
        out[name] = jnp.asarray(drawn.astype(out[name].dtype))
    for name, factor in factors.items():
        out[name] = (out[name] * factor).astype(out[name].dtype)
    return out
```

```python
from contextlib import ExitStack

import concourse.bass as bass
from concourse import mybir

F32 = mybir.dt.float32
F32R = mybir.dt.float32r
BF16 = mybir.dt.bfloat16
I32 = mybir.dt.int32
ALU = mybir.AluOpType
ACT = mybir.ActivationFunctionType
AX = mybir.AxisListType

B, T, D = 32, 256, 128
NH, DH = 16, 8
P = 128
TT = T // P
NT = B * TT
HG = 4
G = NH // HG
SLOT = 32
NE, CAP, HID = 8, 160, 512
HC = HID // P
N = B * T
SLOTS = NE * CAP
HALF = CAP // 2
NEG = -1.0e30
SM_SCALE = float(DH) ** -0.5
EPS = 1e-5
MAGIC = 1597463007.0
LAST = 2 * N


class Steps:

    def __init__(self, eng, sem, base):
        self.eng, self.sem, self.value = eng, sem, base

    def did(self, ins):
        ins.then_inc(self.sem, 1)
        self.value = self.value + 1

    def wait(self, plain=None):
        self.eng.wait_ge(self.sem, self.value)
        if plain is not None:
            settle(self.eng, plain)


def rsqrt(nc, st, var, y, h, t):
    v = nc.vector
    st.did(v.tensor_scalar(h, var, EPS, None, ALU.add))
    st.wait()
    st.did(v.tensor_scalar(t.bitcast(I32), h.bitcast(I32), 1, None, ALU.arith_shift_right))
    st.wait()
    st.did(v.tensor_scalar(y.bitcast(I32), t.bitcast(I32), -1.0, MAGIC, ALU.mult, ALU.add))
    for _ in range(3):
        st.wait()
        st.did(v.tensor_tensor(t, y, y, ALU.mult))
        st.wait()
        st.did(v.scalar_tensor_tensor(t, t, -0.5, h, ALU.mult, ALU.mult))
        st.wait()
        st.did(v.scalar_tensor_tensor(y, t, 1.5, y, ALU.add, ALU.mult))
    st.wait()


RSQRT_STEPS = 12
ROUTE = 26


CREDIT = 1


def settle(eng, passed):
    eng.sem_inc(passed, 1)


def wait(eng, sem, value):
    if isinstance(value, int) and value <= 0:
        return
    eng.wait_ge(sem, value)


def layer_kernel(nc, x, w_qkvo, bo, cos, sin, masks, eye, router_w, router_b, w1, b1, w2, b2,
                 ow1, ob1, ow2, ob2, tri, rank_table, tokens, idx_init, out, slot_tok, x1_dram):
    ctx = ExitStack()
    with ctx:
        phase1 = ExitStack()

        def sb(name, shape, dt=F32, held=ctx):
            return held.enter_context(nc.sbuf_tensor(name, shape, dt))

        def pb(name, shape, dt=F32):
            return ctx.enter_context(nc.psum_tensor(name, shape, dt))

        def sem(name):
            return ctx.enter_context(nc.semaphore(name))

        x_sb = sb("x_sb", [P, N])
        xn2T = sb("xn2T", [P, N])
        logits = sb("logits", [P, NT, NE])
        w_sb = sb("w_sb", [P, 4 * D])
        bo_sb = sb("bo_sb", [P, D])
        cos_sb = sb("cos_sb", [P, TT, DH])
        sin_sb = sb("sin_sb", [P, TT, DH])
        mask_f = sb("mask_f", [P, 2, 4 * P])
        mask_sb = sb("mask_sb", [P, 2, 4 * P], BF16)
        eye_f = sb("eye_f", [P, P])
        eye_r = sb("eye_r", [P, P], F32R)
        eye_b = sb("eye_b", [P, P], BF16)
        rw_sb = sb("rw_sb", [P, NE])
        rb_sb = sb("rb_sb", [P, NE])

        ow1_sb = sb("ow1_sb", [P, HID])
        ow2_sb = sb("ow2_sb", [P, HC, D])
        ob1_sb = sb("ob1_sb", [P, HC])
        ob2_sb = sb("ob2_sb", [P, D])
        b1_sb = sb("b1_sb", [P, NE, HC])
        b2_sb = sb("b2_sb", [P, NE, D])
        tri_f = sb("tri_f", [P, P])
        rank_c = sb("rank_c", [P, 2, NE])
        tok_id = sb("tok_id", [P, NT], I32)

        xn = sb("xn", [P, TT, D], held=phase1)
        ln_st = sb("ln_st", [P, TT, 6], held=phase1)
        ln_mv = sb("ln_mv", [P, TT, 2], held=phase1)
        ln_y = sb("ln_y", [P, TT], held=phase1)
        ln_h = sb("ln_h", [P, TT], held=phase1)
        ln_t = sb("ln_t", [P, TT], held=phase1)
        xnT = sb("xnT", [P, T], held=phase1)
        rope_c = sb("rope_c", [P, TT, 2 * NH, DH], held=phase1)
        rope_s = sb("rope_s", [P, TT, 2 * NH, DH], held=phase1)
        rope = sb("rope", [P, TT, 2 * NH, DH], held=phase1)
        v_raw = sb("v_raw", [P, TT, NH, DH], held=phase1)
        aug = [sb(f"aug{i}", [P, TT, 2 * NH, SLOT], F32R, held=phase1) for i in range(2)]
        ones_f = sb("ones_f", [P, 2 * TT * NH], held=phase1)
        k_diag = [sb(f"k_diag{i}", [P, G, HG, T], F32R, held=phase1) for i in range(2)]
        qT_max = sb("qT_max", [P, G, T], F32R, held=phase1)
        qT = [sb(f"qT{i}", [P, G, T], F32R, held=phase1) for i in range(2)]
        neg_max = sb("neg_max", [P, TT, NH], held=phase1)
        v_aug = [sb(f"v_aug{i}", [P, TT, NH, SLOT], held=phase1) for i in range(2)]
        NPB = 4
        probs = [sb(f"probs{i}", [P, 3 * P], held=phase1) for i in range(NPB)]
        oT = sb("oT", [P, G, T], held=phase1)
        rden = sb("rden", [P, NH], held=phase1)
        o_tok = sb("o_tok", [P, TT, NH, DH], held=phase1)
        o_tokT = sb("o_tokT", [P, T], held=phase1)
        at = sb("at", [P, TT, D], held=phase1)
        a_st = sb("a_st", [P, TT, 6], held=phase1)
        a_mv = sb("a_mv", [P, TT, 2], held=phase1)
        a_y = sb("a_y", [P, TT], held=phase1)
        a_h = sb("a_h", [P, TT], held=phase1)
        a_t = sb("a_t", [P, TT], held=phase1)
        xn2 = sb("xn2", [P, TT, D], held=phase1)
        xn2T_now = sb("xn2T_now", [P, T], held=phase1)
        phase1.close()

        tri_b = sb("tri_b", [P, P], BF16)
        ones_b = sb("ones_b", [P, P], BF16)
        best = sb("best", [P, NT])
        pick = sb("pick", [P, NT, NE])
        hot = sb("hot", [P, NT, NE])
        hot_b = sb("hot_b", [P, NT, NE], BF16)
        total = sb("total", [P, NE, NT])
        upto = sb("upto", [P, NE, NT])
        zeros = sb("zeros", [P, NT])
        slot_f = sb("slot_f", [P, NT])
        slot_i = sb("slot_i", [P, NT], I32)
        QUAD = 4
        lot_slot = [sb(f"lot_slot{i}", [P, QUAD], I32) for i in range(2)]
        lot_tok = [sb(f"lot_tok{i}", [P, QUAD], I32) for i in range(2)]
        hid = [sb(f"hid{i}", [P, HC, QUAD * P]) for i in range(2)]
        y_sb = sb("y_sb", [P, QUAD, D])
        y_st = sb("y_st", [P, QUAD, 6])
        y_mv = sb("y_mv", [P, QUAD, 2])
        y_y = sb("y_y", [P, QUAD])
        y_h = sb("y_h", [P, QUAD])
        y_t = sb("y_t", [P, QUAD])
        fin = [sb(f"fin{i}", [P, QUAD, D]) for i in range(2)]
        KT = NE * 2
        slot_idx = sb("slot_idx", [HALF, KT], I32)
        xg = sb("xg", [HALF, KT, D])
        g_st = sb("g_st", [HALF, 2, 6])
        g_mv = sb("g_mv", [HALF, 2, 2])
        g_y = sb("g_y", [HALF, 2])
        g_h = sb("g_h", [HALF, 2])
        g_t = sb("g_t", [HALF, 2])
        xgn = sb("xgn", [HALF, 2, D])
        xgT = sb("xgT", [P, CAP])
        w1_sb = [sb(f"w1_sb{i}", [P, HID]) for i in range(2)]
        w2_sb = [sb(f"w2_sb{i}", [P, HC, D]) for i in range(2)]
        hid_e = sb("hid_e", [P, HC, CAP])
        y_e = sb("y_e", [HALF, 2, D])
        res = sb("res", [HALF, KT, D])

        ps_w = pb("ps_w", [P, 2, 512])
        ps_a = [pb(f"ps_a{i}", [P, 512]) for i in range(2)]
        ps_s = [pb(f"ps_s{i}", [P, 512]) for i in range(2)]
        ps_o = pb("ps_o", [P, 512])
        ps_b = pb("ps_b", [P, 512])

        consts_in = sem("consts_in")
        x_first = sem("x_first")
        x_rest = sem("x_rest")
        consts_ready = sem("consts_ready")
        pads_ready = sem("pads_ready")
        ones_ready = sem("ones_ready")
        lnx_step = sem("lnx_step")
        xt_done = sem("xt_done")
        xnT_ready = sem("xnT_ready")
        qkv_done = sem("qkv_done")
        rope_parts = sem("rope_parts")
        rope_ready = sem("rope_ready")
        vraw_ready = sem("vraw_ready")
        hi_ready = sem("hi_ready")
        aug_ready = sem("aug_ready")
        kt_done = sem("kt_done")
        kdiag_ready = sem("kdiag_ready")
        qt_done = sem("qt_done")
        qtmax_ready = sem("qtmax_ready")
        sa_done = sem("sa_done")
        max_done = sem("max_done")
        shift_step = sem("shift_step")
        qT_ready = sem("qT_ready")
        vaug_ready = sem("vaug_ready")
        s_done = sem("s_done")
        exp_done = sem("exp_done")
        sel_done = sem("sel_done")
        pv_done = sem("pv_done")
        oT_ready = sem("oT_ready")
        otok_psum = sem("otok_psum")
        norm_step = sem("norm_step")
        otokT_done = sem("otokT_done")
        otokT_ready = sem("otokT_ready")
        y_done = sem("y_done")
        attn_step = sem("attn_step")
        xn2t_done = sem("xn2t_done")
        xn2T_ready = sem("xn2T_ready")
        xn2T_kept = sem("xn2T_kept")
        lg_psum = sem("lg_psum")
        lg_ready = sem("lg_ready")
        dve_passed = sem("dve_passed")
        pool_passed = sem("pool_passed")
        late_in = sem("late_in")
        table_init = sem("table_init")
        x1_stored = sem("x1_stored")
        route_step = sem("route_step")
        rank_psum = sem("rank_psum")
        lot_ready = sem("lot_ready")
        scattered = [sem(f"scattered{i}") for i in range(2)]
        h_done = sem("h_done")
        hid_ready = sem("hid_ready")
        yov_done = sem("yov_done")
        over_step = sem("over_step")
        out_stored = [sem(f"out_stored{i}") for i in range(2)]
        idx_in = sem("idx_in")
        xg_clear = sem("xg_clear")
        gathered = sem("gathered")
        weights_in = [sem(f"weights_in{i}") for i in range(2)]
        gnorm_step = sem("gnorm_step")
        gT_psum = sem("gT_psum")
        xgT_ready = sem("xgT_ready")
        he_done = sem("he_done")
        hid_e_ready = sem("hid_e_ready")
        ye_done = sem("ye_done")
        res_step = sem("res_step")
        res_stored = sem("res_stored")

        LNX = 2 * TT + RSQRT_STEPS + TT
        ATT = 1 + 2 * TT + RSQRT_STEPS + TT + 1 + 2 * TT + RSQRT_STEPS + TT
        STEPS2 = NT // QUAD
        OVER = 1 + 2 * QUAD + RSQRT_STEPS + QUAD + 1
        GNORM = 2 + 2 + RSQRT_STEPS + 2
        RES = 1 + GNORM + 1
        h_bank = [ps_w[:, 0], ps_w[:, 1], ps_a[0][:], ps_a[1][:]]
        y_bank = [ps_s[0][:], ps_s[1][:]]
        block = ctx.enter_context(nc.Block())

        @block.sync
        def _(sp):
            xt = x.rearrange("(n p) d -> p n d", p=P)
            xs = x_sb[:].rearrange("p (n d) -> p n d", d=D)
            first = 3 * TT
            sp.dma_start(xs[:, 0:first, :], xt[:, 0:first, :]).then_inc(x_first, 16)
            for dst, src in ((w_sb[:], w_qkvo), (bo_sb[:], bo), (cos_sb[:], cos), (sin_sb[:], sin),
                             (mask_f[:], masks), (eye_f[:], eye), (rw_sb[:], router_w),
                             (rb_sb[:], router_b)):
                sp.dma_start(dst, src).then_inc(consts_in, 16)
            sp.dma_start(xs[:, first:, :], xt[:, first:, :]).then_inc(x_rest, 16)
            sp.dma_start(slot_tok, idx_init).then_inc(table_init, 16)
            for dst, src in ((ow1_sb[:], ow1), (ow2_sb[:], ow2.rearrange("(m p) d -> p m d", p=P)),
                             (ob1_sb[:], ob1), (ob2_sb[:], ob2), (b1_sb[:], b1), (b2_sb[:], b2),
                             (tri_f[:], tri), (rank_c[:], rank_table), (tok_id[:], tokens)):
                sp.dma_start(dst, src).then_inc(late_in, 16)
            sp.wait_ge(attn_step, ATT * B)
            sp.dma_start(x1_dram.rearrange("(n p) d -> p n d", p=P), xs).then_inc(x1_stored, 16)
            ot = out.rearrange("(n p) d -> p n d", p=P)
            with sp.Fori(0, STEPS2 // 2) as k:
                for par in range(2):
                    i = k * 2 + par
                    sp.wait_ge(over_step, OVER * (i + 1) + CREDIT)
                    sp.dma_start(ot[:, bass.ds(i * QUAD, QUAD), :], fin[par][:])\
                        .then_inc(out_stored[par], 16)
            for par in range(2):
                sp.wait_ge(scattered[par], 16 * NT // 2)
            sp.dma_start(slot_idx[:], slot_tok.rearrange("(k p) o -> p (k o)", p=HALF),
                         allow_slow_non_contiguous=True)\
                .then_inc(idx_in, 16)
            with sp.Fori(0, NE // 2 - 1) as k:
                for par in range(2):
                    e = k * 2 + par
                    sp.wait_ge(ye_done, e + 1)
                    sp.dma_start(w1_sb[par][:].unsqueeze(1), w1.rearrange("e p n -> p e n")[:, bass.ds(e + 2, 1), :])\
                        .then_inc(weights_in[par], 16)
                    sp.dma_start(w2_sb[par][:].unsqueeze(1),
                                 w2.rearrange("e (m p) d -> p e m d", p=P)[:, bass.ds(e + 2, 1), :, :])\
                        .then_inc(weights_in[par], 16)

        @block.vector
        def _(dve):
            v = nc.vector
            dve.wait_ge(consts_in, 16 * 8)
            v.tensor_copy(eye_r[:], eye_f[:])
            v.tensor_copy(eye_b[:], eye_f[:])
            v.tensor_copy(mask_sb[:], mask_f[:]).then_inc(consts_ready, 1)

            def ln_x(b):
                if isinstance(b, int):
                    dve.wait_ge(x_first if b < 3 else x_rest, 16)
                else:
                    dve.wait_ge(x_rest, 16)
                st = Steps(dve, lnx_step, LNX * b)
                for t in range(TT):
                    st.did(v.bn_stats(out=ln_st[:, t], in_=x_sb[:, bass.ds(b * T + t * D, D)]))
                st.wait(dve_passed)
                for t in range(TT):
                    st.did(v.bn_aggr(out=ln_mv[:, t], in_=ln_st[:, t]))
                st.wait()
                rsqrt(nc, st, ln_mv[:, :, 1], ln_y[:], ln_h[:], ln_t[:])
                wait(dve, xt_done, b)
                for t in range(TT):
                    st.did(v.tensor_scalar(xn[:, t], x_sb[:, bass.ds(b * T + t * D, D)],
                                           ln_mv[:, t, 0:1], ln_y[:, t:t + 1],
                                           ALU.subtract, ALU.mult))

            def rotary(b):
                dve.wait_ge(qkv_done, b + 1)
                wait(dve, rope_ready, b)
                qk = ps_w[:, :, 0:2 * D].rearrange("p t (h d) -> p t h d", d=DH)
                full = [P, TT, 2 * NH, DH]
                half = [P, TT, 2 * NH, DH // 2]
                h = DH // 2
                v.tensor_tensor(rope_c[:], qk, cos_sb[:].unsqueeze(2).broadcast_to(full), ALU.mult)
                v.tensor_tensor(rope_s[:, :, :, 0:h], qk[:, :, :, h:],
                                sin_sb[:, :, 0:h].unsqueeze(2).broadcast_to(half), ALU.mult)
                v.tensor_tensor(rope_s[:, :, :, h:], qk[:, :, :, 0:h],
                                sin_sb[:, :, h:].unsqueeze(2).broadcast_to(half),
                                ALU.mult).then_inc(rope_parts, 1)

            def evict_qT_max(b):
                dve.wait_ge(qt_done, 2 * b + 1)
                v.tensor_copy(qT_max[:].rearrange("p g t -> p (g t)"),
                              ps_w[:].rearrange("p a n -> p (a n)")).then_inc(qtmax_ready, 1)

            def evict_qT(b, par):
                dve.wait_ge(qt_done, 2 * b + 2)
                v.tensor_copy(qT[par][:].rearrange("p g t -> p (g t)"),
                              ps_w[:].rearrange("p a n -> p (a n)")).then_inc(qT_ready, 1)

            def row_max(b, u):
                g, k = divmod(u, 3)
                dve.wait_ge(sa_done, 12 * b + u + 1)
                if k == 0:
                    o = neg_max[:, 0, HG * g:HG * g + HG]
                    i = ps_a[u % 2][:].rearrange("p (h k) -> p h k", h=HG)
                else:
                    o = neg_max[:, 1, HG * g + 2 * (k - 1):HG * g + 2 * k]
                    i = ps_a[u % 2][:].rearrange("p (h k) -> p h k", h=2)
                v.tensor_reduce(o, i, AX.X, ALU.max, negate=True).then_inc(max_done, 1)

            def shift(b, par):
                dve.wait_ge(max_done, 12 * b + 12)
                st = Steps(dve, shift_step, 2 * b)
                st.did(v.tensor_copy(aug[par][:, :, 0:NH, 24], neg_max[:]))
                st.wait()
                st.did(v.tensor_tensor(aug[par][:, :, 0:NH, 25], neg_max[:],
                                       aug[par][:, :, 0:NH, 24].bitcast(F32), ALU.subtract))

            def divide(b, t):
                dve.wait_ge(otok_psum, 2 * b + t + 1)
                st = Steps(dve, norm_step, 4 * b + 2 * t)
                o = ps_b[:].rearrange("p (h s) -> p h s", s=SLOT)
                if t == 0:
                    wait(dve, otokT_done, b)
                st.did(v.reciprocal(rden[:], o[:, :, DH]))
                st.wait()
                st.did(v.tensor_tensor(o_tok[:, t], o[:, :, 0:DH],
                                       rden[:].unsqueeze(2).broadcast_to([P, NH, DH]), ALU.mult))

            def norm_of(st, src, dst, stats, mv):
                settle(dve, dve_passed)
                for t in range(TT):
                    st.did(v.bn_stats(out=stats[:, t], in_=src(t)))
                st.wait(dve_passed)
                for t in range(TT):
                    st.did(v.bn_aggr(out=mv[:, t], in_=stats[:, t]))
                st.wait()
                rsqrt(nc, st, mv[:, :, 1], a_y[:], a_h[:], a_t[:])
                for t in range(TT):
                    st.did(v.tensor_scalar(dst[:, t], src(t), mv[:, t, 0:1], a_y[:, t:t + 1],
                                           ALU.subtract, ALU.mult))

            def attn_norm(b):
                dve.wait_ge(y_done, b + 1)
                st = Steps(dve, attn_step, ATT * b)
                st.did(v.tensor_tensor(at[:], ps_b[:, 0:T].rearrange("p (t d) -> p t d", t=TT),
                                       bo_sb[:].unsqueeze(1).broadcast_to([P, TT, D]), ALU.add))
                st.wait()
                norm_of(st, lambda t: at[:, t], at, a_st, a_mv)
                st.wait()
                row = x_sb[:, bass.ds(b * T, T)]
                st.did(v.tensor_tensor(row, row, at[:].rearrange("p t d -> p (t d)"), ALU.add))
                return st

            def ffn_norm(b, st):
                st.wait()
                wait(dve, xn2t_done, b)
                norm_of(st, lambda t: x_sb[:, bass.ds(b * T + t * D, D)], xn2, a_st, a_mv)

            def logits_out(b):
                dve.wait_ge(lg_psum, b + 1)
                v.tensor_tensor(logits[:, bass.ds(b * TT, TT), :],
                                ps_b[:, 0:TT * NE].rearrange("p (t e) -> p t e", e=NE),
                                rb_sb[:].unsqueeze(1).broadcast_to([P, TT, NE]),
                                ALU.add).then_inc(lg_ready, 1)

            def step(n, f1, f2, b2, par):
                if f1:
                    ln_x(n + 2)
                if f2:
                    evict_qT_max(n + 1)
                if b2:
                    divide(n - 1, 0)
                if f2:
                    for u in range(0, 2):
                        row_max(n + 1, u)
                if b2:
                    divide(n - 1, 1)
                if f2:
                    for u in range(2, 6):
                        row_max(n + 1, u)
                if f1:
                    rotary(n + 2)
                if f2:
                    for u in range(6, 8):
                        row_max(n + 1, u)
                if b2:
                    st = attn_norm(n - 1)
                if f2:
                    for u in range(8, 12):
                        row_max(n + 1, u)
                    shift(n + 1, 1 - par)
                if b2:
                    ffn_norm(n - 1, st)
                if f2:
                    evict_qT(n + 1, 1 - par)
                if b2:
                    logits_out(n - 1)

            steady(dve, lambda n, par, f1, f2, b1, b2: step(n, f1, f2, b2, par))

            dve.wait_ge(late_in, 16 * 9)
            dve.wait_ge(lg_ready, B)
            st = Steps(dve, route_step, 0)
            st.did(v.memset(ones_b[:], 1.0))
            st.did(v.memset(zeros[:], 0.0))
            st.did(v.tensor_copy(tri_b[:], tri_f[:]))
            per_tile = lambda a: a.unsqueeze(2).broadcast_to([P, NT, NE])
            per_expert = lambda a: a.unsqueeze(1).broadcast_to([P, NT, NE])
            st.did(v.tensor_reduce(best[:], logits[:], AX.X, ALU.max))
            st.wait()
            st.did(v.tensor_tensor(pick[:], logits[:], per_tile(best[:]), ALU.is_ge))
            st.wait()
            st.did(v.tensor_tensor(pick[:], pick[:], per_expert(rank_c[:, 0]), ALU.mult))
            st.wait()
            st.did(v.tensor_reduce(best[:], pick[:], AX.X, ALU.max))
            st.wait()
            st.did(v.tensor_tensor(hot[:], pick[:], per_tile(best[:]), ALU.is_equal))
            st.wait()
            st.did(v.tensor_copy(hot_b[:], hot[:]))
            dve.wait_ge(rank_psum, 1)
            st.did(v.tensor_copy(total[:], ps_b[:].rearrange("p (n e) -> p e n", e=NE)))
            st.wait()
            for e in range(NE):
                st.did(v.tensor_tensor_scan(upto[:, e], total[:, e], zeros[:], 0.0, ALU.add, ALU.add))
            st.wait()
            st.did(v.tensor_tensor(upto[:], upto[:], total[:], ALU.subtract))
            st.wait()
            st.did(v.tensor_tensor(pick[:], ps_o[:].rearrange("p (n e) -> p n e", e=NE),
                                   upto[:].rearrange("p e n -> p n e"), ALU.add))
            st.wait()
            lg = logits[:]
            st.did(v.tensor_scalar(lg, pick[:], float(CAP) + 0.5, 1.0e5, ALU.is_gt, ALU.mult))
            st.wait()
            st.did(v.tensor_tensor(pick[:], pick[:], lg, ALU.add))
            st.wait()
            st.did(v.tensor_tensor(pick[:], pick[:], per_expert(rank_c[:, 1]), ALU.add))
            st.wait()
            st.did(v.tensor_tensor(pick[:], pick[:], hot[:], ALU.mult))
            st.wait()
            st.did(v.tensor_reduce(slot_f[:], pick[:], AX.X, ALU.add))
            st.wait()
            st.did(v.tensor_copy(slot_i[:], slot_f[:]))
            assert st.value == ROUTE

            def layer_norm(st, src, dst, stats, mv, y, h, t, n):
                for k in range(n):
                    st.did(v.bn_stats(out=stats[:, k], in_=src[:, k]))
                st.wait(dve_passed)
                for k in range(n):
                    st.did(v.bn_aggr(out=mv[:, k], in_=stats[:, k]))
                st.wait()
                rsqrt(nc, st, mv[:, :, 1], y[:], h[:], t[:])
                for k in range(n):
                    st.did(v.tensor_scalar(dst[:, k], src[:, k], mv[:, k, 0:1], y[:, k:k + 1],
                                           ALU.subtract, ALU.mult))

            dve.sem_inc(over_step, CREDIT)
            for par in range(2):
                dve.sem_inc(out_stored[par], 16)
            with dve.Fori(0, STEPS2 // 2) as k2:
                for par in range(2):
                    i = k2 * 2 + par
                    dve.wait_ge(over_step, OVER * i + CREDIT)
                    dve.wait_ge(yov_done, i + 3)
                    st = Steps(dve, over_step, OVER * i + CREDIT)
                    st.did(v.tensor_tensor(y_sb[:], y_bank[par].rearrange("p (n d) -> p n d", d=D),
                                           ob2_sb[:].unsqueeze(1).broadcast_to([P, QUAD, D]), ALU.add))
                    st.wait(dve_passed)
                    layer_norm(st, y_sb, y_sb, y_st, y_mv, y_y, y_h, y_t, QUAD)
                    st.wait()
                    dve.wait_ge(out_stored[par], k2 * 16 + 16)
                    st.did(v.tensor_tensor(fin[par][:].rearrange("p n d -> p (n d)"),
                                           x_sb[:, bass.ds(i * QUAD * D, QUAD * D)],
                                           y_sb[:].rearrange("p n d -> p (n d)"), ALU.add))

            dve.wait_ge(gathered, 16 * KT)
            dve.sem_inc(res_step, CREDIT)
            with dve.Fori(0, NE // 2) as k2:
                for par in range(2):
                    e = k2 * 2 + par
                    dve.wait_ge(res_step, RES * e + CREDIT)
                    dve.wait_ge(gT_psum, e + CREDIT)
                    settle(dve, dve_passed)
                    st = Steps(dve, gnorm_step, GNORM * e)
                    tiles = xg[:, bass.ds(e * 2, 2), :]
                    layer_norm(st, tiles, xgn, g_st, g_mv, g_y, g_h, g_t, 2)
                    dve.wait_ge(gnorm_step, GNORM * e + GNORM)
                    dve.wait_ge(ye_done, e + 1)
                    st = Steps(dve, res_step, RES * e + CREDIT)
                    st.did(v.tensor_tensor(y_e[:], ps_b[0:HALF, 0:2 * D].rearrange("p (n d) -> p n d", d=D),
                                           b2_sb[0:HALF, bass.ds(e, 1), :].broadcast_to([HALF, 2, D]),
                                           ALU.add))
                    st.wait(dve_passed)
                    layer_norm(st, y_e, y_e, g_st, g_mv, g_y, g_h, g_t, 2)
                    st.wait()
                    st.did(v.tensor_tensor(res[:, bass.ds(e * 2, 2), :], tiles, y_e[:], ALU.add))

        @block.gpsimd
        def _(pool):
            gp = nc.gpsimd
            zero = pool.to_reg(0.0)
            for i in range(2):
                gp.memset(aug[i][:].bitcast(F32), 0.0).then_inc(pads_ready, 1)
                gp.memset(k_diag[i][:].bitcast(F32), 0.0).then_inc(pads_ready, 1)
                gp.memset(v_aug[i][:], 0.0).then_inc(pads_ready, 1)
            gp.memset(ones_f[:], 1.0).then_inc(pads_ready, 1)
            pool.wait_ge(pads_ready, 7)
            for i in range(2):
                gp.tensor_copy(aug[i][:, :, NH:, 24:26],
                               ones_f[:].rearrange("p (t h s) -> p t h s", t=TT, s=2))
                gp.memset(v_aug[i][:, :, :, DH:DH + 1], 1.0)
            gp.memset(rope_c[:], 0.0).then_inc(ones_ready, 1)

            def sum_rope(b):
                pool.wait_ge(rope_parts, b + 1)
                wait(pool, hi_ready, b)
                wait(pool, aug_ready, b)
                gp.tensor_tensor(rope[:], rope_c[:], rope_s[:], ALU.add).then_inc(rope_ready, 1)

            def low_parts(b, par):
                pool.wait_ge(hi_ready, b + 1)
                a = aug[par]
                gp.tensor_tensor(a[:, :, 0:NH, 16:24], rope[:, :, 0:NH],
                                 a[:, :, 0:NH, 0:8].bitcast(F32), ALU.subtract)
                gp.tensor_tensor(a[:, :, NH:, 8:16], rope[:, :, NH:],
                                 a[:, :, NH:, 0:8].bitcast(F32), ALU.subtract)
                gp.memset(a[:, :, 0:NH, 24:26].bitcast(F32), 0.0).then_inc(aug_ready, 1)

            def keep_v(b, par):
                pool.wait_ge(vraw_ready, b + 1)
                wait(pool, pv_done, NH * (b - 1))
                settle(pool, pool_passed)
                gp.tensor_copy(v_aug[par][:, :, :, 0:DH], v_raw[:]).then_inc(vaug_ready, 1)

            def causal(b, j):
                J = NH * b + j
                pool.wait_ge(exp_done, J + 1)
                settle(pool, pool_passed)
                pr = probs[j % NPB]
                d = pr[:, 0:2 * P].rearrange("p (a q) -> p a q", a=2)
                gp.affine_select(out=d, in_=d, compare_op=ALU.is_ge, fill=zero, base=0,
                                 pattern=[[0, 2], [1, P]], channel_multiplier=-1)
                e = pr[:, 2 * P:3 * P]
                gp.affine_select(out=e, in_=e, compare_op=ALU.is_ge, fill=zero, base=-1,
                                 pattern=[[-1, P]], channel_multiplier=1).then_inc(sel_done, 1)

            def keep_xn2T(b):
                pool.wait_ge(xn2T_ready, b + 1)
                settle(pool, pool_passed)
                gp.tensor_copy(xn2T[:, bass.ds(b * T, T)], xn2T_now[:]).then_inc(xn2T_kept, 1)

            def step(n, par, f1, f2, b1, b2):
                for j in range(NH):
                    if b1:
                        causal(n, j)
                    if f2 and j == 3:
                        keep_v(n + 1, 1 - par)
                    if f1 and j == 9:
                        sum_rope(n + 2)
                    if f1 and j == 11:
                        low_parts(n + 2, par)
                    if b2 and j == 15:
                        keep_xn2T(n - 1)

            steady(pool, step)

            pool.wait_ge(table_init, 16)
            pool.wait_ge(route_step, ROUTE)
            def scatter_lot(k2, par):
                i = k2 * 2 + par
                if not isinstance(k2, int):
                    pool.wait_ge(scattered[par], k2 * (16 * QUAD))
                    settle(pool, pool_passed)
                gp.tensor_copy(lot_slot[par][:], slot_i[:, bass.ds(i * QUAD, QUAD)])
                gp.tensor_copy(lot_tok[par][:], tok_id[:, bass.ds(i * QUAD, QUAD)])\
                    .then_inc(lot_ready, 1)
                pool.wait_ge(lot_ready, i + 1)
                settle(pool, pool_passed)
                for c in range(QUAD):
                    gp.indirect_dma_start(
                        out=slot_tok, out_offset=bass.IndirectOffsetOnAxis(ap=lot_slot[par][:, c:c + 1], axis=0),
                        in_=lot_tok[par][:, c:c + 1], in_offset=None, bounds_check=SLOTS - 1,
                        oob_is_err=False).then_inc(scattered[par], 16)

            for par in range(2):
                scatter_lot(0, par)
            with pool.Fori(1, NT // (2 * QUAD)) as k2:
                for par in range(2):
                    scatter_lot(k2, par)

            gp.memset(xg[:], 0.0).then_inc(xg_clear, 1)
            pool.wait_ge(xg_clear, 1)
            pool.wait_ge(idx_in, 16)
            pool.wait_ge(x1_stored, 16)
            for k in range(KT):
                gp.indirect_dma_start(
                    out=xg[:, k, :], out_offset=None, in_=x1_dram,
                    in_offset=bass.IndirectOffsetOnAxis(ap=slot_idx[:, k:k + 1], axis=0),
                    bounds_check=N - 1, oob_is_err=False).then_inc(gathered, 16)
            for par in range(2):
                pool.wait_ge(out_stored[par], 16 * STEPS2 // 2 + 16)
            for k in range(KT):
                if k % 2 == 0:
                    pool.wait_ge(res_step, RES * (k // 2 + 1) + CREDIT)
                gp.indirect_dma_start(
                    out=out, out_offset=bass.IndirectOffsetOnAxis(ap=slot_idx[:, k:k + 1], axis=0),
                    in_=res[:, k, :], in_offset=None, bounds_check=N - 1,
                    oob_is_err=False).then_inc(res_stored, 16)
            pool.wait_ge(res_stored, 16 * KT)

        @block.scalar
        def _(act):
            s = nc.scalar

            def evict_xnT(b):
                act.wait_ge(xt_done, b + 1)
                wait(act, qkv_done, b)
                s.copy(xnT[:], ps_w[:, 0, 0:T]).then_inc(xnT_ready, 1)

            def evict_v(b):
                act.wait_ge(rope_parts, b + 1)
                wait(act, vaug_ready, b)
                s.copy(v_raw[:], ps_w[:, :, 2 * D:3 * D].rearrange("p t (h d) -> p t h d", d=DH))\
                    .then_inc(vraw_ready, 1)

            def high_parts(b, par):
                act.wait_ge(rope_ready, b + 1)
                a = aug[par]
                s.copy(a[:, :, :, 0:8], rope[:])
                s.copy(a[:, :, 0:NH, 8:16], rope[:, :, 0:NH])
                s.copy(a[:, :, NH:, 16:24], rope[:, :, NH:]).then_inc(hi_ready, 1)

            def spread_k(b, par):
                act.wait_ge(kt_done, b + 1)
                for c in range(HG):
                    q = slice(32 * c, 32 * c + 32)
                    last = s.copy(k_diag[par][q, :, c, :],
                                  ps_w[q].rearrange("p a (g t) -> p (a g) t", t=T))
                last.then_inc(kdiag_ready, 1)

            def exps(b, j):
                J = NH * b + j
                act.wait_ge(s_done, J + 1)
                wait(act, pv_done, J - NPB + 1)
                s.activation(probs[j % NPB][:], ps_s[j % 2][:, P:4 * P], ACT.Exp,
                             scale=SM_SCALE).then_inc(exp_done, 1)

            def evict_oT(b, g):
                act.wait_ge(pv_done, NH * b + HG * (g + 1))
                s.copy(oT[:, g, :], ps_o[:, 0:T]).then_inc(oT_ready, 1)

            def evict_otokT(b):
                act.wait_ge(otokT_done, b + 1)
                s.copy(o_tokT[:], ps_b[:, 0:T]).then_inc(otokT_ready, 1)

            def evict_xn2T(b):
                act.wait_ge(xn2t_done, b + 1)
                wait(act, xn2T_kept, b)
                s.copy(xn2T_now[:], ps_b[:, 0:T]).then_inc(xn2T_ready, 1)

            def step(n, par, f1, f2, b1, b2):
                for j in range(NH):
                    if b1:
                        exps(n, j)
                    if j == 0 and f2:
                        spread_k(n + 1, 1 - par)
                    if j == 2 and b2:
                        evict_oT(n - 1, 3)
                    if b1 and j in (6, 10, 14):
                        evict_oT(n, (j - 6) // 4)
                    if f1 and j == 7:
                        evict_xnT(n + 2)
                    if b2 and j == 8:
                        evict_otokT(n - 1)
                    if f1 and j == 9:
                        evict_v(n + 2)
                    if f1 and j == 10:
                        high_parts(n + 2, par)
                    if b2 and j == 14:
                        evict_xn2T(n - 1)

            act.wait_ge(ones_ready, 1)
            steady(act, step)

            act.wait_ge(late_in, 16 * 9)
            with act.Fori(0, STEPS2 // 2) as k2:
                for par in range(2):
                    i = k2 * 2 + par
                    act.wait_ge(yov_done, i + 1)
                    for m in range(HC):
                        act.wait_ge(h_done, i * HC + m + 1)
                        s.activation(hid[par][:, m, :], h_bank[m], ACT.Relu,
                                     bias=ob1_sb[:, m:m + 1]).then_inc(hid_ready, 1)

            def load(e, par):
                act.dma_start(w1_sb[par][:], w1[e]).then_inc(weights_in[par], 16)
                act.dma_start(w2_sb[par][:], w2[e].rearrange("(m p) d -> p m d", p=P))\
                    .then_inc(weights_in[par], 16)

            for par in range(2):
                load(par, par)
            act.sem_inc(hid_e_ready, CREDIT)
            with act.Fori(0, NE // 2) as k2:
                for par in range(2):
                    e = k2 * 2 + par
                    act.wait_ge(gT_psum, e + 1 + CREDIT)
                    s.copy(xgT[:], ps_w[:, 0, 0:CAP]).then_inc(xgT_ready, 1)
                    for m in range(HC):
                        act.wait_ge(he_done, e * HC + m + 1)
                        s.activation(hid_e[:, m, :], h_bank[m][:, 0:CAP], ACT.Relu,
                                     bias=b1_sb[:, bass.ds(e, 1), m]).then_inc(hid_e_ready, 1)

        @block.tensor
        def _(pe):
            mm = nc.tensor.matmul
            tr = nc.tensor.transpose
            w_flat = ps_w[:].rearrange("p a n -> p (a n)")

            def xn_T(b):
                pe.wait_ge(lnx_step, LNX * (b + 1))
                wait(pe, qtmax_ready, b)
                for t in range(TT):
                    last = tr(ps_w[:, 0, t * P:(t + 1) * P], xn[:, t], eye_f[:])
                last.then_inc(xt_done, 1)

            def qkv(b):
                pe.wait_ge(xnT_ready, b + 1)
                for t in range(TT):
                    last = mm(ps_w[:, t, 0:3 * D], xnT[:, t * P:(t + 1) * P], w_sb[:, 0:3 * D])
                last.then_inc(qkv_done, 1)

            def k_T(b, par):
                pe.wait_ge(aug_ready, b + 1)
                wait(pe, qT_ready, b)
                for g in range(G):
                    for t in range(TT):
                        last = tr(w_flat[:, g * T + t * P:g * T + t * P + P].bitcast(F32R),
                                  aug[par][:, t, NH + HG * g:NH + HG * g + HG, :]
                                  .rearrange("p h s -> p (h s)"), eye_r[:])
                last.then_inc(kt_done, 1)

            def q_T(b, par, again):
                if again:
                    pe.wait_ge(shift_step, 2 * b + 2)
                    wait(pe, rope_parts, b + 2 if not isinstance(b, int) else min(b + 2, B))
                    wait(pe, vraw_ready, b + 2 if not isinstance(b, int) else min(b + 2, B))
                else:
                    pe.wait_ge(kdiag_ready, b + 1)
                for g in range(G):
                    for t in range(TT):
                        last = tr(w_flat[:, g * T + t * P:g * T + t * P + P].bitcast(F32R),
                                  aug[par][:, t, HG * g:HG * g + HG, :]
                                  .rearrange("p h s -> p (h s)"), eye_r[:])
                last.then_inc(qt_done, 1)

            def max_scores(b, par, u):
                g, k = divmod(u, 3)
                if u == 0:
                    pe.wait_ge(qtmax_ready, b + 1)
                wait(pe, max_done, 12 * b + u - 1)
                bank = ps_a[u % 2][:]
                if k == 0:
                    keys = k_diag[par][:, g, :, 0:P]
                    q = qT_max[:, g, 0:P]
                else:
                    keys = k_diag[par][:, g, 2 * (k - 1):2 * k, :]
                    q = qT_max[:, g, P:T]
                mm(bank, eye_b[:], mask_sb[:, min(k, 1), :], start=True, stop=False)
                mm(bank, q, keys, start=False, stop=True).then_inc(sa_done, 1)

            def scores(b, par, j):
                J = NH * b + j
                g, c = divmod(j, HG)
                if j == 0:
                    pe.wait_ge(qT_ready, b + 1)
                wait(pe, exp_done, J - 1)
                bank = ps_s[j % 2]
                mm(bank[:, 0:T], k_diag[par][:, g, c, P:T], qT[par][:, g, :])
                mm(bank[:, T:2 * T], k_diag[par][:, g, c, 0:P], qT[par][:, g, :])\
                    .then_inc(s_done, 1)

            def values(b, par, j):
                J = NH * b + j
                g, c = divmod(j, HG)
                if j == 0:
                    pe.wait_ge(vaug_ready, b + 1)
                pe.wait_ge(sel_done, J + 1)
                if c == 0:
                    wait(pe, oT_ready, G * b + g)
                pr = probs[j % NPB]
                q = slice(32 * c, 32 * c + 32)
                mm(ps_o[q, 0:T], v_aug[par][:, 0, j, :], pr[:, P:3 * P], start=True, stop=False,
                   tile_position=(0, 32 * c))
                mm(ps_o[q, P:T], v_aug[par][:, 1, j, :], pr[:, 0:P], start=False, stop=True,
                   tile_position=(0, 32 * c)).then_inc(pv_done, 1)

            def o_T(b, t):
                if t == 0:
                    pe.wait_ge(oT_ready, G * b + G)
                    wait(pe, lg_ready, b)
                else:
                    pe.wait_ge(norm_step, 4 * b + 2)
                for g in range(G):
                    last = tr(ps_b[:, g * P:(g + 1) * P], oT[:, g, t * P:(t + 1) * P], eye_f[:])
                last.then_inc(otok_psum, 1)

            def otok_T(b):
                pe.wait_ge(norm_step, 4 * b + 4)
                for t in range(TT):
                    last = tr(ps_b[:, t * P:(t + 1) * P],
                              o_tok[:, t].rearrange("p h d -> p (h d)"), eye_f[:])
                last.then_inc(otokT_done, 1)

            def project(b):
                pe.wait_ge(otokT_ready, b + 1)
                for t in range(TT):
                    last = mm(ps_b[:, t * P:(t + 1) * P], o_tokT[:, t * P:(t + 1) * P],
                              w_sb[:, 3 * D:4 * D])
                last.then_inc(y_done, 1)

            def xn2_T(b):
                pe.wait_ge(attn_step, ATT * (b + 1))
                for t in range(TT):
                    last = tr(ps_b[:, t * P:(t + 1) * P], xn2[:, t], eye_f[:])
                last.then_inc(xn2t_done, 1)

            def route(b):
                pe.wait_ge(xn2T_ready, b + 1)
                for t in range(TT):
                    last = mm(ps_b[:, t * NE:(t + 1) * NE], xn2T_now[:, t * P:(t + 1) * P], rw_sb[:])
                last.then_inc(lg_psum, 1)

            def step(n, par, f1, f2, b1, b2):
                units = {4: (0, 1), 5: (2, 3), 6: (4,), 7: (5,), 8: (6,), 9: (7,), 10: (8, 9),
                         11: (10,), 12: (11,)}
                for j in range(NH):
                    if b1:
                        scores(n, par, j)
                    if f2 and j == 0:
                        k_T(n + 1, 1 - par)
                    if j >= 3 and b1:
                        values(n, par, j - 3)
                    if j < 3 and b2:
                        values(n - 1, 1 - par, j + 13)
                    if f2 and j == 3:
                        q_T(n + 1, 1 - par, False)
                    if b2 and j == 3:
                        o_T(n - 1, 0)
                    if f2:
                        for u in units.get(j, ()):
                            max_scores(n + 1, 1 - par, u)
                    if b2 and j == 5:
                        o_T(n - 1, 1)
                    if f1 and j == 6:
                        xn_T(n + 2)
                    if b2 and j == 7:
                        otok_T(n - 1)
                    if f1 and j == 8:
                        qkv(n + 2)
                    if b2 and j == 9:
                        project(n - 1)
                    if f2 and j == 13:
                        q_T(n + 1, 1 - par, True)
                    if b2 and j == 13:
                        xn2_T(n - 1)
                    if b2 and j == 15:
                        route(n - 1)

            pe.wait_ge(consts_ready, 1)
            pe.wait_ge(ones_ready, 1)
            steady(pe, step)

            pe.wait_ge(route_step, 9)
            mm(ps_o[:], tri_b[:], hot_b[:].rearrange("p n e -> p (n e)"))
            mm(ps_b[:], ones_b[:], hot_b[:].rearrange("p n e -> p (n e)")).then_inc(rank_psum, 1)

            def hidden(i):
                for m in range(HC):
                    wait(pe, hid_ready, i * HC + m - HC + 1)
                    mm(h_bank[m], ow1_sb[:, m * P:(m + 1) * P], xn2T[:, bass.ds(i * QUAD * P, QUAD * P)])\
                        .then_inc(h_done, 1)

            pe.sem_inc(yov_done, 2)

            def over(i, par):
                pe.wait_ge(hid_ready, i * HC + HC)
                if not isinstance(i, int) or i >= 2:
                    pe.wait_ge(over_step, (i - 2) * OVER + 1 + CREDIT)
                for c in range(QUAD):
                    for m in range(HC):
                        last = mm(y_bank[par][:, c * D:(c + 1) * D], hid[par][:, m, c * P:(c + 1) * P],
                                  ow2_sb[:, m, :], start=(m == 0), stop=(m == HC - 1))
                last.then_inc(yov_done, 1)

            pe.wait_ge(late_in, 16 * 9)
            pe.wait_ge(xn2T_kept, B)
            for i in range(3):
                hidden(i)
                if i:
                    over(i - 1, (i - 1) % 2)
            with pe.Fori(0, (STEPS2 - 4) // 2) as k2:
                for c in (3, 4):
                    hidden(k2 * 2 + c)
                    over(k2 * 2 + (c - 1), (c - 1) % 2)
            hidden(STEPS2 - 1)
            for i in (STEPS2 - 2, STEPS2 - 1):
                over(i, i % 2)

            pe.wait_ge(hid_ready, HC * STEPS2)
            pe.sem_inc(gT_psum, CREDIT)
            with pe.Fori(0, NE // 2) as k2:
                for par in range(2):
                    e = k2 * 2 + par
                    pe.wait_ge(gnorm_step, (e + 1) * GNORM)
                    pe.wait_ge(hid_e_ready, e * HC + CREDIT)
                    for t in range(2):
                        last = tr(ps_w[:, 0, t * HALF:(t + 1) * HALF], xgn[:, t], eye_f[0:HALF, 0:HALF])
                    last.then_inc(gT_psum, 1)
                    pe.wait_ge(weights_in[par], (k2 + 1) * 32)
                    pe.wait_ge(xgT_ready, e + 1)
                    for m in range(HC):
                        mm(h_bank[m][:, 0:CAP], w1_sb[par][:, m * P:(m + 1) * P], xgT[:])\
                            .then_inc(he_done, 1)
                    pe.wait_ge(hid_e_ready, e * HC + HC + CREDIT)
                    pe.wait_ge(res_step, e * RES + CREDIT)
                    for t in range(2):
                        for m in range(HC):
                            last = mm(ps_b[0:HALF, t * D:(t + 1) * D],
                                      hid_e[:, m, t * HALF:(t + 1) * HALF], w2_sb[par][:, m, :],
                                      start=(m == 0), stop=(m == HC - 1))
                    last.then_inc(ye_done, 1)


def steady(eng, step):
    def edge(n):
        step(n, n % 2, 0 <= n + 2 < B, 0 <= n + 1 < B, 0 <= n < B, 0 <= n - 1 < B)

    for n in range(-2, 2):
        edge(n)
    with eng.Fori(0, (B - 6) // 2) as i:
        for k in (2, 3):
            step(i * 2 + k, k % 2, True, True, True, True)
    for n in range(B - 4, B + 1):
        edge(n)


_INS = ("x", "w_qkvo", "bo", "cos", "sin", "masks", "eye", "router_w", "router_b", "w1", "b1", "w2",
        "b2", "ow1", "ob1", "ow2", "ob2", "tri", "rank_table", "tokens", "idx_init")


def shape_tables(np):
    inv = (1.0 / (np.float32(10000.0) ** (np.arange(0, DH, 2, dtype=np.float32) / np.float32(DH)))).astype(np.float32)
    ang = np.arange(T, dtype=np.float32)[:, None] * inv[None, :]
    ang = np.concatenate([ang, ang], -1)
    tile = lambda a: np.ascontiguousarray(a.reshape(TT, P, DH).transpose(1, 0, 2), dtype=np.float32)
    sin = np.sin(ang)
    sin[:, :DH // 2] *= -1.0
    q, k = np.arange(P)[:, None], np.arange(P)[None, :]
    causal = np.where(k <= q, 0.0, NEG)
    window = np.concatenate([np.where(k > q, 0.0, NEG), causal], 1)
    masks = np.stack([np.tile(causal, (1, HG)), np.tile(window, (1, 2))], 1).astype(np.float32)
    return {"cos": tile(np.cos(ang)), "sin": tile(sin), "masks": masks,
            "eye": np.eye(P, dtype=np.float32),
            "rank_table": np.ascontiguousarray(np.broadcast_to(
                np.stack([NE - np.arange(NE), CAP * np.arange(NE) - 1.0])[None], (P, 2, NE)), dtype=np.float32),
            "tokens": np.ascontiguousarray(np.arange(N, dtype=np.int32).reshape(NT, P).T),
            "tri": (q <= k).astype(np.float32),
            "idx_init": np.full((SLOTS, 1), LAST, np.int32)}


def kernel(**inputs):
    import numpy as np
    import concourse.bacc as bacc
    from concourse.bass_utils import run_bass_kernel_spmd

    a = {k.replace("L0_attn_", "").replace("L0_ffn_", ""): np.asarray(v) for k, v in inputs.items()}
    rows = lambda v, n=P: np.ascontiguousarray(np.broadcast_to(v[None], (n, *v.shape)))
    data = shape_tables(np)
    data["x"] = np.ascontiguousarray(a["query"].reshape(N, D))
    data["w_qkvo"] = np.ascontiguousarray(np.concatenate([a[w].T for w in ("Wq", "Wk", "Wv", "Wo")], 1))
    data["bo"] = rows(a["bo"])
    data["router_w"] = a["router_w"]
    data["router_b"] = rows(a["router_b"])
    data["w1"] = a["w1"]
    data["b1"] = np.ascontiguousarray(a["b1"].reshape(NE, HC, P).transpose(2, 0, 1))
    data["w2"] = a["w2"]
    data["b2"] = rows(a["b2"])
    data["ow1"] = a["ow1"]
    data["ob1"] = np.ascontiguousarray(a["ob1"].reshape(HC, P).T)
    data["ow2"] = a["ow2"]
    data["ob2"] = rows(a["ob2"])

    nc = bacc.Bacc("TRN2", target_bir_lowering=False, num_devices=1)
    dram, args = {}, []
    for name in _INS:
        arr = np.ascontiguousarray(data[name])
        dram[f"in_{name}"] = arr
        args.append(nc.dram_tensor(f"in_{name}", arr.shape, mybir.dt.from_np(arr.dtype), kind="ExternalInput").ap())
    out = nc.dram_tensor("out_x", (N, D), F32, kind="ExternalOutput").ap()
    slot_tok = nc.dram_tensor("slot_tok", (SLOTS, 1), I32, kind="Internal").ap()
    x1_dram = nc.dram_tensor("x1_dram", (N, D), F32, kind="Internal").ap()
    layer_kernel(nc, *args, out, slot_tok, x1_dram)
    r = run_bass_kernel_spmd(nc, [dram], core_ids=[0])
    return np.asarray(r.results[0]["out_x"]).reshape(B, T, D)
```

```python
from contextlib import ExitStack

import concourse.bass as bass
from concourse import mybir

F32 = mybir.dt.float32
F32R = mybir.dt.float32r
BF16 = mybir.dt.bfloat16
I32 = mybir.dt.int32
ALU = mybir.AluOpType
ACT = mybir.ActivationFunctionType
AX = mybir.AxisListType

B, T, D = 32, 256, 128
NH, DH = 16, 8
P = 128
TT = T // P
NT = B * TT
HG = 4
G = NH // HG
SLOT = 32
NE, CAP, HID = 8, 160, 512
HC = HID // P
N = B * T
SLOTS = NE * CAP
LNS = 3 * TT
HALF = CAP // 2
NEG = -1.0e30
SM_SCALE = float(DH) ** -0.5
EPS = 1e-5
MAGIC = 1597463007.0
LAST = 2 * N


class Steps:

    def __init__(self, eng, sem, base):
        self.eng, self.sem, self.value = eng, sem, base

    def did(self, ins):
        ins.then_inc(self.sem, 1)
        self.value = self.value + 1

    def skip(self, n):
        self.eng.sem_inc(self.sem, n)
        self.value = self.value + n

    def wait(self, plain=None):
        self.eng.wait_ge(self.sem, self.value)
        if plain is not None:
            settle(self.eng, plain)


def rsqrt(nc, st, var, y, h, t, between=None):
    v = nc.vector
    other = between or (lambda k: None)
    st.did(v.tensor_scalar(h, var, EPS, None, ALU.add))
    other(0)
    st.wait()
    st.did(v.tensor_scalar(t.bitcast(I32), h.bitcast(I32), 1, None, ALU.arith_shift_right))
    other(1)
    st.wait()
    st.did(v.tensor_scalar(y.bitcast(I32), t.bitcast(I32), -1.0, MAGIC, ALU.mult, ALU.add))
    other(2)
    for k in range(3):
        st.wait()
        st.did(v.tensor_tensor(t, y, y, ALU.mult))
        other(3 * k + 3)
        st.wait()
        st.did(v.scalar_tensor_tensor(t, t, -0.5, h, ALU.mult, ALU.mult))
        other(3 * k + 4)
        st.wait()
        st.did(v.scalar_tensor_tensor(y, t, 1.5, y, ALU.add, ALU.mult))
        other(3 * k + 5)
    st.wait()


RSQRT_STEPS = 12
ROUTE = 26


CREDIT = 1


def settle(eng, passed):
    eng.sem_inc(passed, 1)


def wait(eng, sem, value):
    if isinstance(value, int) and value <= 0:
        return
    eng.wait_ge(sem, value)


def layer_kernel(nc, x, w_qkvo, bo, cos, sin, masks, eye, router_w, router_b, w1, b1, w2, b2,
                 ow1, ob1, ow2, ob2, tri, rank_table, tokens, idx_init, out, slot_tok, x1_dram):
    ctx = ExitStack()
    with ctx:
        phase1 = ExitStack()

        def sb(name, shape, dt=F32, held=ctx):
            return held.enter_context(nc.sbuf_tensor(name, shape, dt))

        def pb(name, shape, dt=F32):
            return ctx.enter_context(nc.psum_tensor(name, shape, dt))

        def sem(name):
            return ctx.enter_context(nc.semaphore(name))

        x_sb = sb("x_sb", [P, N])
        xn2T = sb("xn2T", [P, N])
        logits = sb("logits", [P, NT, NE])
        w_sb = sb("w_sb", [P, 4 * D])
        bo_sb = sb("bo_sb", [P, D])
        cos_sb = sb("cos_sb", [P, TT, DH])
        sin_sb = sb("sin_sb", [P, TT, DH])
        mask_f = sb("mask_f", [P, 2, 4 * P])
        mask_sb = sb("mask_sb", [P, 2, 4 * P], BF16)
        eye_f = sb("eye_f", [P, P])
        eye_r = sb("eye_r", [P, P], F32R)
        eye_b = sb("eye_b", [P, P], BF16)
        rw_sb = sb("rw_sb", [P, NE])
        rb_sb = sb("rb_sb", [P, NE])

        ow1_sb = sb("ow1_sb", [P, HID])
        ow2_sb = sb("ow2_sb", [P, HC, D])
        ob1_sb = sb("ob1_sb", [P, HC])
        ob2_sb = sb("ob2_sb", [P, D])
        b1_sb = sb("b1_sb", [P, NE, HC])
        b2_sb = sb("b2_sb", [P, NE, D])
        tri_f = sb("tri_f", [P, P])
        rank_c = sb("rank_c", [P, 2, NE])
        tok_id = sb("tok_id", [P, NT], I32)

        xn = sb("xn", [P, TT, D], held=phase1)
        ln_st = sb("ln_st", [P, LNS, 6], held=phase1)
        ln_mv = sb("ln_mv", [P, LNS, 2], held=phase1)
        ln_y = sb("ln_y", [P, LNS], held=phase1)
        ln_h = sb("ln_h", [P, LNS], held=phase1)
        ln_t = sb("ln_t", [P, LNS], held=phase1)
        xnT = sb("xnT", [P, T], held=phase1)
        rope_c = sb("rope_c", [P, TT, 2 * NH, DH], held=phase1)
        rope_s = sb("rope_s", [P, TT, 2 * NH, DH], held=phase1)
        rope = sb("rope", [P, TT, 2 * NH, DH], held=phase1)
        v_raw = sb("v_raw", [P, TT, NH, DH], held=phase1)
        aug = [sb(f"aug{i}", [P, TT, 2 * NH, SLOT], F32R, held=phase1) for i in range(2)]
        ones_f = sb("ones_f", [P, 2 * TT * NH], held=phase1)
        k_diag = [sb(f"k_diag{i}", [P, G, HG, T], F32R, held=phase1) for i in range(2)]
        qT_max = sb("qT_max", [P, G, T], F32R, held=phase1)
        qT = [sb(f"qT{i}", [P, G, T], F32R, held=phase1) for i in range(2)]
        neg_max = sb("neg_max", [P, TT, NH], held=phase1)
        v_aug = [sb(f"v_aug{i}", [P, TT, NH, SLOT], held=phase1) for i in range(2)]
        NPB = 4
        probs = [sb(f"probs{i}", [P, 3 * P], held=phase1) for i in range(NPB)]
        oT = sb("oT", [P, G, T], held=phase1)
        rden = sb("rden", [P, NH], held=phase1)
        o_tok = sb("o_tok", [P, TT, NH, DH], held=phase1)
        o_tokT = sb("o_tokT", [P, T], held=phase1)
        at = sb("at", [P, TT, D], held=phase1)
        xn2 = sb("xn2", [P, TT, D], held=phase1)
        xn2T_now = sb("xn2T_now", [P, T], held=phase1)
        phase1.close()

        tri_b = sb("tri_b", [P, P], BF16)
        ones_b = sb("ones_b", [P, P], BF16)
        best = sb("best", [P, NT])
        pick = sb("pick", [P, NT, NE])
        hot = sb("hot", [P, NT, NE])
        hot_b = sb("hot_b", [P, NT, NE], BF16)
        total = sb("total", [P, NE, NT])
        upto = sb("upto", [P, NE, NT])
        zeros = sb("zeros", [P, NT])
        slot_f = sb("slot_f", [P, NT])
        slot_i = sb("slot_i", [P, NT], I32)
        QUAD = 4
        lot_slot = [sb(f"lot_slot{i}", [P, QUAD], I32) for i in range(2)]
        lot_tok = [sb(f"lot_tok{i}", [P, QUAD], I32) for i in range(2)]
        hid = [sb(f"hid{i}", [P, HC, QUAD * P]) for i in range(2)]
        y_sb = sb("y_sb", [P, QUAD, D])
        y_st = sb("y_st", [P, QUAD, 6])
        y_mv = sb("y_mv", [P, QUAD, 2])
        y_y = sb("y_y", [P, QUAD])
        y_h = sb("y_h", [P, QUAD])
        y_t = sb("y_t", [P, QUAD])
        fin = [sb(f"fin{i}", [P, QUAD, D]) for i in range(2)]
        KT = NE * 2
        slot_idx = sb("slot_idx", [HALF, KT], I32)
        xg = sb("xg", [HALF, KT, D])
        g_st = sb("g_st", [HALF, KT, 6])
        g_mv = sb("g_mv", [HALF, KT, 2])
        g_y = sb("g_y", [HALF, KT])
        g_h = sb("g_h", [HALF, KT])
        g_t = sb("g_t", [HALF, KT])
        xgn = sb("xgn", [HALF, KT, D])
        xgT = sb("xgT", [P, SLOTS])
        NW = 4
        w1_sb = [sb(f"w1_sb{i}", [P, HID]) for i in range(NW)]
        w2_sb = sb("w2_sb", [P, NE, HC, D])
        hid_e = [sb(f"hid_e{i}", [P, HC, CAP]) for i in range(2)]
        y_e = sb("y_e", [HALF, KT, D])

        ps_w = pb("ps_w", [P, 2, 512])
        ps_a = [pb(f"ps_a{i}", [P, 512]) for i in range(2)]
        ps_s = [pb(f"ps_s{i}", [P, 512]) for i in range(2)]
        ps_o = pb("ps_o", [P, 512])
        ps_b = pb("ps_b", [P, 512])

        consts_in = sem("consts_in")
        x_first = sem("x_first")
        x_rest = sem("x_rest")
        consts_ready = sem("consts_ready")
        pads_ready = sem("pads_ready")
        ones_ready = sem("ones_ready")
        norms_step = sem("norms_step")
        xn_ready = sem("xn_ready")
        xn2_ready = sem("xn2_ready")
        xt_done = sem("xt_done")
        xnT_ready = sem("xnT_ready")
        qkv_done = sem("qkv_done")
        rope_parts = sem("rope_parts")
        rope_ready = sem("rope_ready")
        vraw_ready = sem("vraw_ready")
        hi_ready = sem("hi_ready")
        aug_ready = sem("aug_ready")
        kt_done = sem("kt_done")
        kdiag_act = sem("kdiag_act")
        kdiag_dve = sem("kdiag_dve")
        qt_done = sem("qt_done")
        qtmax_ready = sem("qtmax_ready")
        sa_done = sem("sa_done")
        max_done = sem("max_done")
        shift_step = sem("shift_step")
        qT_ready = sem("qT_ready")
        vaug_ready = sem("vaug_ready")
        s_done = sem("s_done")
        exp_done = sem("exp_done")
        sel_done = sem("sel_done")
        pv_done = sem("pv_done")
        oT_ready = sem("oT_ready")
        otok_psum = sem("otok_psum")
        norm_step = sem("norm_step")
        otokT_done = sem("otokT_done")
        otokT_ready = sem("otokT_ready")
        y_done = sem("y_done")
        at_ready = sem("at_ready")
        x1_ready = sem("x1_ready")
        xn2t_done = sem("xn2t_done")
        xn2T_ready = sem("xn2T_ready")
        xn2T_kept = sem("xn2T_kept")
        lg_psum = sem("lg_psum")
        lg_ready = sem("lg_ready")
        dve_passed = sem("dve_passed")
        pool_passed = sem("pool_passed")
        late_in = sem("late_in")
        table_init = sem("table_init")
        x1_stored = sem("x1_stored")
        route_step = sem("route_step")
        rank_psum = sem("rank_psum")
        lot_ready = sem("lot_ready")
        scattered = [sem(f"scattered{i}") for i in range(2)]
        h_done = sem("h_done")
        hid_ready = sem("hid_ready")
        yov_done = sem("yov_done")
        over_step = sem("over_step")
        out_stored = [sem(f"out_stored{i}") for i in range(2)]
        idx_in = sem("idx_in")
        xg_clear = sem("xg_clear")
        gathered = [sem(f"gathered{i}") for i in range(NE * 2 // QUAD)]
        w1_in = [sem(f"w1_in{i}") for i in range(NW)]
        w2_in = sem("w2_in")
        gnorm_step = sem("gnorm_step")
        xgn_ready = sem("xgn_ready")
        gT_psum = sem("gT_psum")
        xgT_ready = sem("xgT_ready")
        he_done = sem("he_done")
        hid_e_ready = sem("hid_e_ready")
        ye_done = sem("ye_done")
        ye_read = sem("ye_read")
        res_step = sem("res_step")
        res_ready = sem("res_ready")
        res_stored = sem("res_stored")

        NORMS = 2 * LNS + RSQRT_STEPS + TT
        STEPS2 = NT // QUAD
        OVER = 1 + 2 * QUAD + RSQRT_STEPS + QUAD + 1
        YE = 3
        h_bank = [ps_w[:, 0], ps_w[:, 1], ps_a[0][:], ps_a[1][:]]
        y_bank = [ps_s[0][:], ps_s[1][:]]
        block = ctx.enter_context(nc.Block())

        @block.sync
        def _(sp):
            xt = x.rearrange("(n p) d -> p n d", p=P)
            xs = x_sb[:].rearrange("p (n d) -> p n d", d=D)
            first = 3 * TT
            sp.dma_start(xs[:, 0:first, :], xt[:, 0:first, :]).then_inc(x_first, 16)
            for dst, src in ((w_sb[:], w_qkvo), (bo_sb[:], bo), (cos_sb[:], cos), (sin_sb[:], sin),
                             (mask_f[:], masks), (eye_f[:], eye), (rw_sb[:], router_w),
                             (rb_sb[:], router_b)):
                sp.dma_start(dst, src).then_inc(consts_in, 16)
            sp.dma_start(xs[:, first:, :], xt[:, first:, :]).then_inc(x_rest, 16)
            sp.dma_start(slot_tok, idx_init).then_inc(table_init, 16)
            for dst, src in ((ow1_sb[:], ow1), (ow2_sb[:], ow2.rearrange("(m p) d -> p m d", p=P)),
                             (ob1_sb[:], ob1), (ob2_sb[:], ob2), (b1_sb[:], b1), (b2_sb[:], b2),
                             (tri_f[:], tri), (rank_c[:], rank_table), (tok_id[:], tokens)):
                sp.dma_start(dst, src).then_inc(late_in, 16)
            sp.wait_ge(x1_ready, B)
            sp.dma_start(x1_dram.rearrange("(n p) d -> p n d", p=P), xs).then_inc(x1_stored, 16)
            sp.wait_ge(lg_ready, B)
            sp.wait_ge(xn2T_kept, B)
            sp.dma_start(w2_sb[:], w2.rearrange("e (m p) d -> p e m d", p=P)).then_inc(w2_in, 16)
            for e in range(NW):
                sp.dma_start(w1_sb[e][:], w1[e]).then_inc(w1_in[e], 16)
            ot = out.rearrange("(n p) d -> p n d", p=P)
            with sp.Fori(0, STEPS2 // 2) as k:
                for par in range(2):
                    i = k * 2 + par
                    sp.wait_ge(over_step, OVER * (i + 1) + CREDIT)
                    sp.dma_start(ot[:, bass.ds(i * QUAD, QUAD), :], fin[par][:])\
                        .then_inc(out_stored[par], 16)
            for e in range(NW, NE):
                sp.wait_ge(he_done, HC * (e - NW + 1))
                sp.dma_start(w1_sb[e - NW][:], w1[e]).then_inc(w1_in[e - NW], 16)

        @block.vector
        def _(dve):
            v = nc.vector
            dve.wait_ge(consts_in, 16 * 8)
            v.tensor_copy(eye_r[:], eye_f[:])
            v.tensor_copy(eye_b[:], eye_f[:])
            v.tensor_copy(mask_sb[:], mask_f[:]).then_inc(consts_ready, 1)

            def rotary(b):
                dve.wait_ge(qkv_done, TT * (b + 1))
                wait(dve, rope_ready, b)
                qk = ps_w[:, :, 0:2 * D].rearrange("p t (h d) -> p t h d", d=DH)
                full = [P, TT, 2 * NH, DH]
                half = [P, TT, 2 * NH, DH // 2]
                h = DH // 2
                v.tensor_tensor(rope_c[:], qk, cos_sb[:].unsqueeze(2).broadcast_to(full), ALU.mult)
                v.tensor_tensor(rope_s[:, :, :, 0:h], qk[:, :, :, h:],
                                sin_sb[:, :, 0:h].unsqueeze(2).broadcast_to(half), ALU.mult)
                v.tensor_tensor(rope_s[:, :, :, h:], qk[:, :, :, 0:h],
                                sin_sb[:, :, h:].unsqueeze(2).broadcast_to(half),
                                ALU.mult).then_inc(rope_parts, 1)

            def spread_k(b, par, half):
                dve.wait_ge(kt_done, 2 * b + half + 1)
                q = slice(32 * (HG - 1), P)
                v.tensor_copy(k_diag[par][q, 2 * half:2 * half + 2, HG - 1, :],
                              ps_w[q, half].rearrange("p (g t) -> p g t", t=T)).then_inc(kdiag_dve, 1)

            def row_max(b, u):
                g, k = divmod(u, 3)
                dve.wait_ge(sa_done, 12 * b + u + 1)
                if k == 0:
                    o = neg_max[:, 0, HG * g:HG * g + HG]
                    i = ps_a[u % 2][:].rearrange("p (h k) -> p h k", h=HG)
                else:
                    o = neg_max[:, 1, HG * g + 2 * (k - 1):HG * g + 2 * k]
                    i = ps_a[u % 2][:].rearrange("p (h k) -> p h k", h=2)
                v.tensor_reduce(o, i, AX.X, ALU.max, negate=True).then_inc(max_done, 1)

            def shift(b, par, half):
                dve.wait_ge(max_done, 12 * b + 6 * half + 6)
                h = slice(NH // 2 * half, NH // 2 * (half + 1))
                st = Steps(dve, shift_step, 4 * b + 2 * half)
                st.did(v.tensor_copy(aug[par][:, :, h, 24], neg_max[:, :, h]))
                st.wait()
                st.did(v.tensor_tensor(aug[par][:, :, h, 25], neg_max[:, :, h],
                                       aug[par][:, :, h, 24].bitcast(F32), ALU.subtract))

            def divide(b, t):
                dve.wait_ge(otok_psum, 2 * b + t + 1)
                st = Steps(dve, norm_step, 4 * b + 2 * t)
                o = ps_b[:].rearrange("p (h s) -> p h s", s=SLOT)
                if t == 0:
                    wait(dve, otokT_done, b)
                st.did(v.reciprocal(rden[:], o[:, :, DH]))
                st.wait()
                st.did(v.tensor_tensor(o_tok[:, t], o[:, :, 0:DH],
                                       rden[:].unsqueeze(2).broadcast_to([P, NH, DH]), ALU.mult))

            def attn_out(b):
                dve.wait_ge(y_done, b + 1)
                wait(dve, x1_ready, b)
                v.tensor_tensor(at[:], ps_b[:, 0:T].rearrange("p (t d) -> p t d", t=TT),
                                bo_sb[:].unsqueeze(1).broadcast_to([P, TT, D]), ALU.add)\
                    .then_inc(at_ready, 1)

            def norms(n, has, after_stats, between):
                tile = lambda b: lambda t: x_sb[:, bass.ds(b * T + t * D, D)]
                parts = [(0, n + 2, tile(n + 2), xn), (1, n - 2, lambda t: at[:, t], at),
                         (2, n - 3, tile(n - 3), xn2)]
                parts = [p for p in parts if has(p[1])]
                if not parts:
                    after_stats()
                    for k in range(RSQRT_STEPS):
                        between(k)
                    return
                st = Steps(dve, norms_step, (n + 2) * NORMS)
                for q, b, src, dst in parts:
                    if q == 0:
                        dve.wait_ge(x_first if isinstance(n, int) and n < 1 else x_rest, 16)
                    else:
                        dve.wait_ge(at_ready if q == 1 else x1_ready, b + 1)
                        settle(dve, dve_passed)
                    for t in range(TT):
                        st.did(v.bn_stats(out=ln_st[:, q * TT + t], in_=src(t)))
                after_stats()
                st.wait(dve_passed)
                for q, b, src, dst in parts:
                    for t in range(TT):
                        st.did(v.bn_aggr(out=ln_mv[:, q * TT + t], in_=ln_st[:, q * TT + t]))
                if len(parts) < 3:
                    st.skip(2 * TT * (3 - len(parts)))
                st.wait()
                cs = slice(parts[0][0] * TT, parts[-1][0] * TT + TT)
                rsqrt(nc, st, ln_mv[:, cs, 1], ln_y[:, cs], ln_h[:, cs], ln_t[:, cs], between)
                for q, b, src, dst in parts:
                    if q == 0:
                        wait(dve, xt_done, b)
                    if q == 2:
                        wait(dve, xn2t_done, b)
                    for t in range(TT):
                        c = q * TT + t
                        ins = v.tensor_scalar(dst[:, t], src(t), ln_mv[:, c, 0:1], ln_y[:, c:c + 1],
                                              ALU.subtract, ALU.mult)
                        if q == 1:
                            st.did(ins)
                    if q != 1:
                        ins.then_inc(xn_ready if q == 0 else xn2_ready, 1)
                if has(n - 2):
                    st.wait()
                    row = x_sb[:, bass.ds((n - 2) * T, T)]
                    v.tensor_tensor(row, row, at[:].rearrange("p t d -> p (t d)"), ALU.add)\
                        .then_inc(x1_ready, 1)
                else:
                    st.skip(TT)

            def logits_out(b):
                dve.wait_ge(lg_psum, b + 1)
                v.tensor_tensor(logits[:, bass.ds(b * TT, TT), :],
                                ps_b[:, 0:TT * NE].rearrange("p (t e) -> p t e", e=NE),
                                rb_sb[:].unsqueeze(1).broadcast_to([P, TT, NE]),
                                ALU.add).then_inc(lg_ready, 1)

            def step(n, par, has):
                f1, f2, b2 = has(n + 2), has(n + 1), has(n - 1)

                def maxima(*units):
                    if f2:
                        for u in units:
                            row_max(n + 1, u)

                def after_stats():
                    if f2:
                        spread_k(n + 1, 1 - par, 0)

                def between(k):
                    if f2 and k == 0:
                        spread_k(n + 1, 1 - par, 1)
                    if k in (7, 10):
                        maxima((k - 7) // 3)
                    if b2 and k == 8:
                        divide(n - 1, 0)

                norms(n, has, after_stats, between)
                maxima(2)
                if b2:
                    divide(n - 1, 1)
                maxima(3, 4)
                if f1:
                    rotary(n + 2)
                maxima(5)
                if f2:
                    shift(n + 1, 1 - par, 0)
                maxima(6)
                if b2:
                    attn_out(n - 1)
                maxima(7, 8, 9, 10)
                if has(n - 3):
                    logits_out(n - 3)
                maxima(11)
                if f2:
                    shift(n + 1, 1 - par, 1)

            steady(dve, step)

            dve.wait_ge(late_in, 16 * 9)
            dve.wait_ge(lg_ready, B)
            st = Steps(dve, route_step, 0)
            st.did(v.memset(ones_b[:], 1.0))
            st.did(v.memset(zeros[:], 0.0))
            st.did(v.tensor_copy(tri_b[:], tri_f[:]))
            per_tile = lambda a: a.unsqueeze(2).broadcast_to([P, NT, NE])
            per_expert = lambda a: a.unsqueeze(1).broadcast_to([P, NT, NE])
            st.did(v.tensor_reduce(best[:], logits[:], AX.X, ALU.max))
            st.wait()
            st.did(v.tensor_tensor(pick[:], logits[:], per_tile(best[:]), ALU.is_ge))
            st.wait()
            st.did(v.tensor_tensor(pick[:], pick[:], per_expert(rank_c[:, 0]), ALU.mult))
            st.wait()
            st.did(v.tensor_reduce(best[:], pick[:], AX.X, ALU.max))
            st.wait()
            st.did(v.tensor_tensor(hot[:], pick[:], per_tile(best[:]), ALU.is_equal))
            st.wait()
            st.did(v.tensor_copy(hot_b[:], hot[:]))
            dve.wait_ge(rank_psum, 1)
            st.did(v.tensor_copy(total[:], ps_b[:].rearrange("p (n e) -> p e n", e=NE)))
            st.wait()
            for e in range(NE):
                st.did(v.tensor_tensor_scan(upto[:, e], total[:, e], zeros[:], 0.0, ALU.add, ALU.add))
            st.wait()
            st.did(v.tensor_tensor(upto[:], upto[:], total[:], ALU.subtract))
            st.wait()
            st.did(v.tensor_tensor(pick[:], ps_o[:].rearrange("p (n e) -> p n e", e=NE),
                                   upto[:].rearrange("p e n -> p n e"), ALU.add))
            st.wait()
            lg = logits[:]
            st.did(v.tensor_scalar(lg, pick[:], float(CAP) + 0.5, 1.0e5, ALU.is_gt, ALU.mult))
            st.wait()
            st.did(v.tensor_tensor(pick[:], pick[:], lg, ALU.add))
            st.wait()
            st.did(v.tensor_tensor(pick[:], pick[:], per_expert(rank_c[:, 1]), ALU.add))
            st.wait()
            st.did(v.tensor_tensor(pick[:], pick[:], hot[:], ALU.mult))
            st.wait()
            st.did(v.tensor_reduce(slot_f[:], pick[:], AX.X, ALU.add))
            st.wait()
            st.did(v.tensor_copy(slot_i[:], slot_f[:]))
            assert st.value == ROUTE

            def layer_norm(st, src, dst, stats, mv, y, h, t, n):
                for k in range(n):
                    st.did(v.bn_stats(out=stats[:, k], in_=src[:, k]))
                st.wait(dve_passed)
                for k in range(n):
                    st.did(v.bn_aggr(out=mv[:, k], in_=stats[:, k]))
                st.wait()
                rsqrt(nc, st, mv[:, :, 1], y[:], h[:], t[:])
                for k in range(n):
                    st.did(v.tensor_scalar(dst[:, k], src[:, k], mv[:, k, 0:1], y[:, k:k + 1],
                                           ALU.subtract, ALU.mult))

            dve.sem_inc(over_step, CREDIT)
            for par in range(2):
                dve.sem_inc(out_stored[par], 16)
            with dve.Fori(0, STEPS2 // 2) as k2:
                for par in range(2):
                    i = k2 * 2 + par
                    dve.wait_ge(over_step, OVER * i + CREDIT)
                    dve.wait_ge(yov_done, i + 3)
                    st = Steps(dve, over_step, OVER * i + CREDIT)
                    st.did(v.tensor_tensor(y_sb[:], y_bank[par].rearrange("p (n d) -> p n d", d=D),
                                           ob2_sb[:].unsqueeze(1).broadcast_to([P, QUAD, D]), ALU.add))
                    st.wait(dve_passed)
                    layer_norm(st, y_sb, y_sb, y_st, y_mv, y_y, y_h, y_t, QUAD)
                    st.wait()
                    dve.wait_ge(out_stored[par], k2 * 16 + 16)
                    st.did(v.tensor_tensor(fin[par][:].rearrange("p n d -> p (n d)"),
                                           x_sb[:, bass.ds(i * QUAD * D, QUAD * D)],
                                           y_sb[:].rearrange("p n d -> p (n d)"), ALU.add))

            st = Steps(dve, gnorm_step, 0)
            for lot in range(KT // QUAD):
                dve.wait_ge(gathered[lot], 16 * QUAD)
                for k in range(lot * QUAD, (lot + 1) * QUAD):
                    st.did(v.bn_stats(out=g_st[:, k], in_=xg[:, k]))
            st.wait()
            for k in range(KT):
                st.did(v.bn_aggr(out=g_mv[:, k], in_=g_st[:, k]))
            st.wait()
            rsqrt(nc, st, g_mv[:, :, 1], g_y[:], g_h[:], g_t[:])
            for k in range(KT):
                v.tensor_scalar(xgn[:, k], xg[:, k], g_mv[:, k, 0:1], g_y[:, k:k + 1],
                                ALU.subtract, ALU.mult).then_inc(xgn_ready, 1)
            dve.sem_inc(ye_read, 2 * YE)
            for half in range(2):
                with dve.Fori(half * 2, half * 2 + 2) as k2:
                    for par in range(2):
                        e = k2 * 2 + par
                        dve.wait_ge(ye_done, e + 3)
                        st = Steps(dve, ye_read, (e + 2) * YE)
                        st.did(v.tensor_tensor(y_e[:, bass.ds(e * 2, 2), :],
                                               y_bank[par][0:HALF, 0:2 * D].rearrange("p (n d) -> p n d", d=D),
                                               b2_sb[0:HALF, bass.ds(e, 1), :].broadcast_to([HALF, 2, D]),
                                               ALU.add))
                        st.wait(dve_passed)
                        for t in range(2):
                            st.did(v.bn_stats(out=g_st[:, bass.ds(e * 2 + t, 1), :],
                                              in_=y_e[:, bass.ds(e * 2 + t, 1), :]))
                dve.wait_ge(ye_read, (half + 1) * YE * NE // 2 + 2 * YE)
                ks = range(half * NE, (half + 1) * NE)
                st = Steps(dve, res_step, half * (2 * NE + RSQRT_STEPS))
                cs = slice(ks[0], ks[-1] + 1)
                for k in ks:
                    st.did(v.bn_aggr(out=g_mv[:, k], in_=g_st[:, k]))
                st.wait()
                rsqrt(nc, st, g_mv[:, cs, 1], g_y[:, cs], g_h[:, cs], g_t[:, cs])
                for k in ks:
                    st.did(v.tensor_scalar(y_e[:, k], y_e[:, k], g_mv[:, k, 0:1], g_y[:, k:k + 1],
                                           ALU.subtract, ALU.mult))
                st.wait()
                v.tensor_tensor(y_e[:, cs], y_e[:, cs], xg[:, cs], ALU.add).then_inc(res_ready, 1)

        @block.gpsimd
        def _(pool):
            gp = nc.gpsimd
            zero = pool.to_reg(0.0)
            for i in range(2):
                gp.memset(aug[i][:].bitcast(F32), 0.0).then_inc(pads_ready, 1)
                gp.memset(k_diag[i][:].bitcast(F32), 0.0).then_inc(pads_ready, 1)
                gp.memset(v_aug[i][:], 0.0).then_inc(pads_ready, 1)
            gp.memset(ones_f[:], 1.0).then_inc(pads_ready, 1)
            pool.wait_ge(pads_ready, 7)
            for i in range(2):
                gp.tensor_copy(aug[i][:, :, NH:, 24:26],
                               ones_f[:].rearrange("p (t h s) -> p t h s", t=TT, s=2))
                gp.memset(v_aug[i][:, :, :, DH:DH + 1], 1.0)
            gp.memset(rope_c[:], 0.0).then_inc(ones_ready, 1)

            def sum_rope(b):
                pool.wait_ge(rope_parts, b + 1)
                wait(pool, hi_ready, b)
                wait(pool, aug_ready, b)
                gp.tensor_tensor(rope[:], rope_c[:], rope_s[:], ALU.add).then_inc(rope_ready, 1)

            def low_parts(b, par):
                pool.wait_ge(hi_ready, b + 1)
                a = aug[par]
                gp.tensor_tensor(a[:, :, 0:NH, 16:24], rope[:, :, 0:NH],
                                 a[:, :, 0:NH, 0:8].bitcast(F32), ALU.subtract)
                gp.tensor_tensor(a[:, :, NH:, 8:16], rope[:, :, NH:],
                                 a[:, :, NH:, 0:8].bitcast(F32), ALU.subtract)
                gp.memset(a[:, :, 0:NH, 24:26].bitcast(F32), 0.0).then_inc(aug_ready, 1)

            def keep_v(b, par):
                pool.wait_ge(vraw_ready, b + 1)
                wait(pool, pv_done, NH * (b - 1))
                settle(pool, pool_passed)
                gp.tensor_copy(v_aug[par][:, :, :, 0:DH], v_raw[:]).then_inc(vaug_ready, 1)

            def causal(b, j):
                J = NH * b + j
                pool.wait_ge(exp_done, J + 1)
                settle(pool, pool_passed)
                pr = probs[j % NPB]
                d = pr[:, 0:2 * P].rearrange("p (a q) -> p a q", a=2)
                gp.affine_select(out=d, in_=d, compare_op=ALU.is_ge, fill=zero, base=0,
                                 pattern=[[0, 2], [1, P]], channel_multiplier=-1)
                e = pr[:, 2 * P:3 * P]
                gp.affine_select(out=e, in_=e, compare_op=ALU.is_ge, fill=zero, base=-1,
                                 pattern=[[-1, P]], channel_multiplier=1).then_inc(sel_done, 1)

            def keep_xn2T(b):
                pool.wait_ge(xn2T_ready, b + 1)
                settle(pool, pool_passed)
                gp.tensor_copy(xn2T[:, bass.ds(b * T, T)], xn2T_now[:]).then_inc(xn2T_kept, 1)

            def step(n, par, has):
                for j in range(NH):
                    if has(n):
                        causal(n, j)
                    if has(n - 3) and j == 13:
                        keep_xn2T(n - 3)
                    if has(n + 1) and j == 3:
                        keep_v(n + 1, 1 - par)
                    if has(n + 2) and j == 10:
                        sum_rope(n + 2)
                    if has(n + 2) and j == 12:
                        low_parts(n + 2, par)

            steady(pool, step)

            pool.wait_ge(table_init, 16)
            pool.wait_ge(route_step, ROUTE)
            def scatter_lot(k2, par):
                i = k2 * 2 + par
                if not isinstance(k2, int):
                    pool.wait_ge(scattered[par], k2 * (16 * QUAD))
                    settle(pool, pool_passed)
                gp.tensor_copy(lot_slot[par][:], slot_i[:, bass.ds(i * QUAD, QUAD)])
                gp.tensor_copy(lot_tok[par][:], tok_id[:, bass.ds(i * QUAD, QUAD)])\
                    .then_inc(lot_ready, 1)
                pool.wait_ge(lot_ready, i + 1)
                settle(pool, pool_passed)
                for c in range(QUAD):
                    gp.indirect_dma_start(
                        out=slot_tok, out_offset=bass.IndirectOffsetOnAxis(ap=lot_slot[par][:, c:c + 1], axis=0),
                        in_=lot_tok[par][:, c:c + 1], in_offset=None, bounds_check=SLOTS - 1,
                        oob_is_err=False).then_inc(scattered[par], 16)

            for par in range(2):
                scatter_lot(0, par)
            with pool.Fori(1, NT // (2 * QUAD)) as k2:
                for par in range(2):
                    scatter_lot(k2, par)

            gp.memset(xg[:], 0.0).then_inc(xg_clear, 1)
            pool.wait_ge(xg_clear, 1)
            for par in range(2):
                pool.wait_ge(scattered[par], 16 * NT // 2)
            gp.dma_start(slot_idx[:], slot_tok.rearrange("(k p) o -> p (k o)", p=HALF),
                         allow_slow_non_contiguous=True).then_inc(idx_in, 16)
            pool.wait_ge(idx_in, 16)
            pool.wait_ge(x1_stored, 16)
            for k in range(KT):
                gp.indirect_dma_start(
                    out=xg[:, k, :], out_offset=None, in_=x1_dram,
                    in_offset=bass.IndirectOffsetOnAxis(ap=slot_idx[:, k:k + 1], axis=0),
                    bounds_check=N - 1, oob_is_err=False).then_inc(gathered[k // QUAD], 16)
            for par in range(2):
                pool.wait_ge(out_stored[par], 16 * STEPS2 // 2 + 16)
            for k in range(KT):
                if k % NE == 0:
                    pool.wait_ge(res_ready, k // NE + 1)
                gp.indirect_dma_start(
                    out=out, out_offset=bass.IndirectOffsetOnAxis(ap=slot_idx[:, k:k + 1], axis=0),
                    in_=y_e[:, k, :], in_offset=None, bounds_check=N - 1,
                    oob_is_err=False).then_inc(res_stored, 16)
            pool.wait_ge(res_stored, 16 * KT)

        @block.scalar
        def _(act):
            s = nc.scalar

            def evict_xnT(b):
                act.wait_ge(xt_done, b + 1)
                wait(act, qkv_done, TT * b)
                s.copy(xnT[:], ps_w[:, 0, 0:T]).then_inc(xnT_ready, 1)

            def evict_v(b):
                act.wait_ge(rope_parts, b + 1)
                wait(act, vaug_ready, b)
                s.copy(v_raw[:], ps_w[:, :, 2 * D:3 * D].rearrange("p t (h d) -> p t h d", d=DH))\
                    .then_inc(vraw_ready, 1)

            def high_parts(b, par):
                act.wait_ge(rope_ready, b + 1)
                a = aug[par]
                s.copy(a[:, :, :, 0:8], rope[:])
                s.copy(a[:, :, 0:NH, 8:16], rope[:, :, 0:NH])
                s.copy(a[:, :, NH:, 16:24], rope[:, :, NH:]).then_inc(hi_ready, 1)

            def spread_k(b, par, half, c):
                act.wait_ge(kt_done, 2 * b + half + 1)
                q = slice(32 * c, 32 * c + 32)
                last = s.copy(k_diag[par][q, 2 * half:2 * half + 2, c, :],
                              ps_w[q, half].rearrange("p (g t) -> p g t", t=T))
                if c == HG - 2:
                    last.then_inc(kdiag_act, 1)

            def evict_q(b, half, dst, shifted, ready):
                act.wait_ge(qt_done, 4 * b + 2 * shifted + half + 1)
                s.copy(dst[:, 2 * half:2 * half + 2, :],
                       ps_w[:, half].rearrange("p (g t) -> p g t", t=T)).then_inc(ready, 1)

            def exps(b, j):
                J = NH * b + j
                act.wait_ge(s_done, J + 1)
                wait(act, pv_done, J - NPB + 1)
                s.activation(probs[j % NPB][:], ps_s[j % 2][:, P:4 * P], ACT.Exp,
                             scale=SM_SCALE).then_inc(exp_done, 1)

            def evict_oT(b, g):
                act.wait_ge(pv_done, NH * b + HG * (g + 1))
                s.copy(oT[:, g, :], ps_o[:, 0:T]).then_inc(oT_ready, 1)

            def evict_otokT(b):
                act.wait_ge(otokT_done, b + 1)
                s.copy(o_tokT[:], ps_b[:, 0:T]).then_inc(otokT_ready, 1)

            def evict_xn2T(b):
                act.wait_ge(xn2t_done, b + 1)
                wait(act, xn2T_kept, b)
                s.copy(xn2T_now[:], ps_b[:, 0:T]).then_inc(xn2T_ready, 1)

            def step(n, par, has):
                spread = {0: ((0, 0), (0, 1)), 1: ((0, 2),), 2: ((1, 0), (1, 1)), 3: ((1, 2),)}
                f1, f2, b2 = has(n + 2), has(n + 1), has(n - 1)
                for j in range(NH):
                    if has(n):
                        exps(n, j)
                    if b2 and j == 2:
                        evict_oT(n - 1, 3)
                    if f2 and j == 3:
                        evict_q(n + 1, 0, qT_max, 0, qtmax_ready)
                    if f2:
                        for half, c in spread.get(j, ()):
                            spread_k(n + 1, 1 - par, half, c)
                    if f2 and j == 5:
                        evict_q(n + 1, 1, qT_max, 0, qtmax_ready)
                    if f1 and j == 6:
                        evict_xnT(n + 2)
                    if has(n) and j in (6, 10, 14):
                        evict_oT(n, (j - 6) // 4)
                    if b2 and j == 8:
                        evict_otokT(n - 1)
                    if f1 and j == 9:
                        evict_v(n + 2)
                    if f1 and j == 11:
                        high_parts(n + 2, par)
                    if f2 and j == 12:
                        evict_q(n + 1, 0, qT[1 - par], 1, qT_ready)
                    if has(n - 3) and j == 12:
                        evict_xn2T(n - 3)
                if f2:
                    evict_q(n + 1, 1, qT[1 - par], 1, qT_ready)

            act.wait_ge(ones_ready, 1)
            steady(act, step)

            act.wait_ge(late_in, 16 * 9)
            with act.Fori(0, STEPS2 // 2) as k2:
                for par in range(2):
                    i = k2 * 2 + par
                    act.wait_ge(yov_done, i + 1)
                    for m in range(HC):
                        act.wait_ge(h_done, i * HC + m + 1)
                        s.activation(hid[par][:, m, :], h_bank[m], ACT.Relu,
                                     bias=ob1_sb[:, m:m + 1]).then_inc(hid_ready, 1)

            for lot in range(KT // QUAD):
                act.wait_ge(gT_psum, lot + 1)
                s.copy(xgT[:, lot * QUAD * HALF:(lot + 1) * QUAD * HALF],
                       h_bank[lot][:, 0:QUAD * HALF]).then_inc(xgT_ready, 1)
            act.sem_inc(hid_e_ready, HC)
            with act.Fori(0, NE // 2) as k2:
                for par in range(2):
                    e = k2 * 2 + par
                    act.wait_ge(ye_done, e + 1)
                    for m in range(HC):
                        act.wait_ge(he_done, e * HC + m + 1)
                        s.activation(hid_e[par][:, m, :], h_bank[m][:, 0:CAP], ACT.Relu,
                                     bias=b1_sb[:, bass.ds(e, 1), m]).then_inc(hid_e_ready, 1)

        @block.tensor
        def _(pe):
            mm = nc.tensor.matmul
            tr = nc.tensor.transpose
            w_flat = ps_w[:].rearrange("p a n -> p (a n)")

            def xn_T(b):
                pe.wait_ge(xn_ready, b + 1)
                wait(pe, qtmax_ready, 2 * b - 1)
                for t in range(TT):
                    last = tr(ps_w[:, 0, t * P:(t + 1) * P], xn[:, t], eye_f[:])
                last.then_inc(xt_done, 1)

            def qkv(b, t):
                if t == 0:
                    pe.wait_ge(xnT_ready, b + 1)
                else:
                    wait(pe, qtmax_ready, 2 * b)
                mm(ps_w[:, t, 0:3 * D], xnT[:, t * P:(t + 1) * P], w_sb[:, 0:3 * D])\
                    .then_inc(qkv_done, 1)

            def aug_T(par, first, half):
                for g in (2 * half, 2 * half + 1):
                    for t in range(TT):
                        last = tr(w_flat[:, g * T + t * P:g * T + t * P + P].bitcast(F32R),
                                  aug[par][:, t, first + HG * g:first + HG * g + HG, :]
                                  .rearrange("p h s -> p (h s)"), eye_r[:])
                return last

            def k_T(b, par, half):
                pe.wait_ge(aug_ready, b + 1)
                wait(pe, qT_ready, 2 * b - 1 + half)
                aug_T(par, NH, half).then_inc(kt_done, 1)

            def q_T(b, par, half, shifted):
                if shifted:
                    pe.wait_ge(shift_step, 4 * b + 2 * half + 2)
                    after = b + 2 if not isinstance(b, int) else min(b + 2, B)
                    pe.wait_ge(rope_parts, after)
                    pe.wait_ge(vraw_ready, after)
                else:
                    pe.wait_ge(kdiag_act, 2 * b + half + 1)
                    pe.wait_ge(kdiag_dve, 2 * b + half + 1)
                aug_T(par, 0, half).then_inc(qt_done, 1)

            def max_scores(b, par, u):
                g, k = divmod(u, 3)
                if u in (0, 6):
                    pe.wait_ge(qtmax_ready, 2 * b + 1 + u // 6)
                wait(pe, max_done, 12 * b + u - 1)
                bank = ps_a[u % 2][:]
                if k == 0:
                    keys = k_diag[par][:, g, :, 0:P]
                    q = qT_max[:, g, 0:P]
                else:
                    keys = k_diag[par][:, g, 2 * (k - 1):2 * k, :]
                    q = qT_max[:, g, P:T]
                mm(bank, eye_b[:], mask_sb[:, min(k, 1), :], start=True, stop=False)
                mm(bank, q, keys, start=False, stop=True).then_inc(sa_done, 1)

            def scores(b, par, j):
                J = NH * b + j
                g, c = divmod(j, HG)
                if j in (0, NH // 2):
                    pe.wait_ge(qT_ready, 2 * b + 1 + j // (NH // 2))
                wait(pe, exp_done, J - 1)
                bank = ps_s[j % 2]
                mm(bank[:, 0:T], k_diag[par][:, g, c, P:T], qT[par][:, g, :])
                mm(bank[:, T:2 * T], k_diag[par][:, g, c, 0:P], qT[par][:, g, :])\
                    .then_inc(s_done, 1)

            def values(b, par, j):
                J = NH * b + j
                g, c = divmod(j, HG)
                if j == 0:
                    pe.wait_ge(vaug_ready, b + 1)
                pe.wait_ge(sel_done, J + 1)
                if c == 0:
                    wait(pe, oT_ready, G * b + g)
                pr = probs[j % NPB]
                q = slice(32 * c, 32 * c + 32)
                mm(ps_o[q, 0:T], v_aug[par][:, 0, j, :], pr[:, P:3 * P], start=True, stop=False,
                   tile_position=(0, 32 * c))
                mm(ps_o[q, P:T], v_aug[par][:, 1, j, :], pr[:, 0:P], start=False, stop=True,
                   tile_position=(0, 32 * c)).then_inc(pv_done, 1)

            def o_T(b, t):
                if t == 0:
                    pe.wait_ge(oT_ready, G * b + G)
                    wait(pe, lg_ready, b - 2)
                else:
                    pe.wait_ge(norm_step, 4 * b + 2)
                for g in range(G):
                    last = tr(ps_b[:, g * P:(g + 1) * P], oT[:, g, t * P:(t + 1) * P], eye_f[:])
                last.then_inc(otok_psum, 1)

            def otok_T(b):
                pe.wait_ge(norm_step, 4 * b + 4)
                for t in range(TT):
                    last = tr(ps_b[:, t * P:(t + 1) * P],
                              o_tok[:, t].rearrange("p h d -> p (h d)"), eye_f[:])
                last.then_inc(otokT_done, 1)

            def project(b):
                pe.wait_ge(otokT_ready, b + 1)
                for t in range(TT):
                    last = mm(ps_b[:, t * P:(t + 1) * P], o_tokT[:, t * P:(t + 1) * P],
                              w_sb[:, 3 * D:4 * D])
                last.then_inc(y_done, 1)

            def xn2_T(b):
                pe.wait_ge(xn2_ready, b + 1)
                pe.wait_ge(at_ready, min(b + 3, B) if isinstance(b, int) else b + 3)
                for t in range(TT):
                    last = tr(ps_b[:, t * P:(t + 1) * P], xn2[:, t], eye_f[:])
                last.then_inc(xn2t_done, 1)

            def route(b):
                pe.wait_ge(xn2T_ready, b + 1)
                for t in range(TT):
                    last = mm(ps_b[:, t * NE:(t + 1) * NE], xn2T_now[:, t * P:(t + 1) * P], rw_sb[:])
                last.then_inc(lg_psum, 1)

            def step(n, par, has):
                f1, f2, b2 = has(n + 2), has(n + 1), has(n - 1)
                for j in range(NH):
                    if has(n):
                        scores(n, par, j)
                    if b2 and j in (3, 5):
                        o_T(n - 1, (j - 3) // 2)
                    if j >= 3 and has(n):
                        values(n, par, j - 3)
                    if j < 3 and b2:
                        values(n - 1, 1 - par, j + 13)
                    if f2 and j in (0, 1):
                        k_T(n + 1, 1 - par, j)
                    if f2 and j in (2, 4):
                        q_T(n + 1, 1 - par, (j - 2) // 2, False)
                    if f2 and j >= 3:
                        for u in ((j - 3,) if j < 15 else ()):
                            max_scores(n + 1, 1 - par, u)
                    if f1 and j == 6:
                        xn_T(n + 2)
                    if f1 and j in (7, 8):
                        qkv(n + 2, j - 7)
                    if b2 and j == 7:
                        otok_T(n - 1)
                    if b2 and j == 9:
                        project(n - 1)
                    if f2 and j == 11:
                        q_T(n + 1, 1 - par, 0, True)
                    if has(n - 3) and j == 11:
                        xn2_T(n - 3)
                    if has(n - 3) and j == 13:
                        route(n - 3)
                if f2:
                    q_T(n + 1, 1 - par, 1, True)

            pe.wait_ge(consts_ready, 1)
            pe.wait_ge(ones_ready, 1)
            steady(pe, step)

            def hidden(i):
                for m in range(HC):
                    wait(pe, hid_ready, i * HC + m - HC + 1)
                    mm(h_bank[m], ow1_sb[:, m * P:(m + 1) * P], xn2T[:, bass.ds(i * QUAD * P, QUAD * P)])\
                        .then_inc(h_done, 1)

            pe.sem_inc(yov_done, 2)

            def over(i, par):
                pe.wait_ge(hid_ready, i * HC + HC)
                if not isinstance(i, int) or i >= 2:
                    pe.wait_ge(over_step, (i - 2) * OVER + 1 + CREDIT)
                for c in range(QUAD):
                    for m in range(HC):
                        last = mm(y_bank[par][:, c * D:(c + 1) * D], hid[par][:, m, c * P:(c + 1) * P],
                                  ow2_sb[:, m, :], start=(m == 0), stop=(m == HC - 1))
                last.then_inc(yov_done, 1)

            pe.wait_ge(late_in, 16 * 9)
            pe.wait_ge(xn2T_kept, B)
            for i in range(3):
                hidden(i)
                if i:
                    over(i - 1, (i - 1) % 2)
                else:
                    pe.wait_ge(route_step, 9)
                    one_hot = hot_b[:].rearrange("p n e -> p (n e)")
                    mm(ps_o[:], tri_b[:], one_hot)
                    mm(ps_b[:], ones_b[:], one_hot).then_inc(rank_psum, 1)
            with pe.Fori(0, (STEPS2 - 4) // 2) as k2:
                for c in (3, 4):
                    hidden(k2 * 2 + c)
                    over(k2 * 2 + (c - 1), (c - 1) % 2)
            hidden(STEPS2 - 1)
            for i in (STEPS2 - 2, STEPS2 - 1):
                over(i, i % 2)

            pe.wait_ge(hid_ready, HC * STEPS2)
            for lot in range(KT // QUAD):
                pe.wait_ge(xgn_ready, (lot + 1) * QUAD)
                for c in range(QUAD):
                    last = tr(h_bank[lot][:, c * HALF:(c + 1) * HALF], xgn[:, lot * QUAD + c],
                              eye_f[0:HALF, 0:HALF])
                last.then_inc(gT_psum, 1)
            pe.wait_ge(w2_in, 16)
            pe.wait_ge(xgT_ready, KT // QUAD)
            pe.wait_ge(over_step, OVER * STEPS2 + CREDIT)
            pe.sem_inc(ye_done, 2)

            def expert_hidden(k, c):
                e = k * NW + c
                pe.wait_ge(w1_in[c], k * 16 + 16)
                for m in range(HC):
                    pe.wait_ge(hid_e_ready, e * HC + m - HC + 1 + HC)
                    mm(h_bank[m][:, 0:CAP], w1_sb[c][:, m * P:(m + 1) * P],
                       xgT[:, bass.ds(e * CAP, CAP)]).then_inc(he_done, 1)

            def expert_out(k, c):
                e = k * NW + c
                pe.wait_ge(hid_e_ready, e * HC + HC + HC)
                pe.wait_ge(ye_read, e * YE - 2 * YE + 1 + 2 * YE)
                for t in range(2):
                    for m in range(HC):
                        last = mm(y_bank[c % 2][0:HALF, t * D:(t + 1) * D],
                                  hid_e[c % 2][:, m, t * HALF:(t + 1) * HALF],
                                  w2_sb[:, bass.ds(e, 1), m, :],
                                  start=(m == 0), stop=(m == HC - 1))
                last.then_inc(ye_done, 1)

            with pe.Fori(0, NE // NW) as k:
                for c in range(NW):
                    expert_hidden(k, c)
                    if c:
                        expert_out(k, c - 1)
                expert_out(k, NW - 1)


def steady(eng, step):
    def edge(n):
        step(n, n % 2, lambda b: 0 <= b < B)

    for n in range(-2, 3):
        edge(n)
    with eng.Fori(0, (B - 6) // 2) as i:
        for k in (3, 4):
            step(i * 2 + k, k % 2, lambda b: True)
    for n in range(B - 3, B + 3):
        edge(n)


_INS = ("x", "w_qkvo", "bo", "cos", "sin", "masks", "eye", "router_w", "router_b", "w1", "b1", "w2",
        "b2", "ow1", "ob1", "ow2", "ob2", "tri", "rank_table", "tokens", "idx_init")


def shape_tables(np):
    inv = (1.0 / (np.float32(10000.0) ** (np.arange(0, DH, 2, dtype=np.float32) / np.float32(DH)))).astype(np.float32)
    ang = np.arange(T, dtype=np.float32)[:, None] * inv[None, :]
    ang = np.concatenate([ang, ang], -1)
    tile = lambda a: np.ascontiguousarray(a.reshape(TT, P, DH).transpose(1, 0, 2), dtype=np.float32)
    sin = np.sin(ang)
    sin[:, :DH // 2] *= -1.0
    q, k = np.arange(P)[:, None], np.arange(P)[None, :]
    causal = np.where(k <= q, 0.0, NEG)
    window = np.concatenate([np.where(k > q, 0.0, NEG), causal], 1)
    masks = np.stack([np.tile(causal, (1, HG)), np.tile(window, (1, 2))], 1).astype(np.float32)
    return {"cos": tile(np.cos(ang)), "sin": tile(sin), "masks": masks,
            "eye": np.eye(P, dtype=np.float32),
            "rank_table": np.ascontiguousarray(np.broadcast_to(
                np.stack([NE - np.arange(NE), CAP * np.arange(NE) - 1.0])[None], (P, 2, NE)), dtype=np.float32),
            "tokens": np.ascontiguousarray(np.arange(N, dtype=np.int32).reshape(NT, P).T),
            "tri": (q <= k).astype(np.float32),
            "idx_init": np.full((SLOTS, 1), LAST, np.int32)}


def kernel(**inputs):
    import numpy as np
    import concourse.bacc as bacc
    from concourse.bass_utils import run_bass_kernel_spmd

    a = {k.replace("L0_attn_", "").replace("L0_ffn_", ""): np.asarray(v) for k, v in inputs.items()}
    rows = lambda v, n=P: np.ascontiguousarray(np.broadcast_to(v[None], (n, *v.shape)))
    data = shape_tables(np)
    data["x"] = np.ascontiguousarray(a["query"].reshape(N, D))
    data["w_qkvo"] = np.ascontiguousarray(np.concatenate([a[w].T for w in ("Wq", "Wk", "Wv", "Wo")], 1))
    data["bo"] = rows(a["bo"])
    data["router_w"] = a["router_w"]
    data["router_b"] = rows(a["router_b"])
    data["w1"] = a["w1"]
    data["b1"] = np.ascontiguousarray(a["b1"].reshape(NE, HC, P).transpose(2, 0, 1))
    data["w2"] = a["w2"]
    data["b2"] = rows(a["b2"])
    data["ow1"] = a["ow1"]
    data["ob1"] = np.ascontiguousarray(a["ob1"].reshape(HC, P).T)
    data["ow2"] = a["ow2"]
    data["ob2"] = rows(a["ob2"])

    nc = bacc.Bacc("TRN2", target_bir_lowering=False, num_devices=1)
    dram, args = {}, []
    for name in _INS:
        arr = np.ascontiguousarray(data[name])
        dram[f"in_{name}"] = arr
        args.append(nc.dram_tensor(f"in_{name}", arr.shape, mybir.dt.from_np(arr.dtype), kind="ExternalInput").ap())
    out = nc.dram_tensor("out_x", (N, D), F32, kind="ExternalOutput").ap()
    slot_tok = nc.dram_tensor("slot_tok", (SLOTS, 1), I32, kind="Internal").ap()
    x1_dram = nc.dram_tensor("x1_dram", (N, D), F32, kind="Internal").ap()
    layer_kernel(nc, *args, out, slot_tok, x1_dram)
    r = run_bass_kernel_spmd(nc, [dram], core_ids=[0])
    return np.asarray(r.results[0]["out_x"]).reshape(B, T, D)
```

```python
from contextlib import ExitStack

import concourse.bass as bass
from concourse import mybir

F32 = mybir.dt.float32
F32R = mybir.dt.float32r
BF16 = mybir.dt.bfloat16
I32 = mybir.dt.int32
ALU = mybir.AluOpType
ACT = mybir.ActivationFunctionType
AX = mybir.AxisListType

B, T, D = 32, 256, 128
NH, DH = 16, 8
P = 128
TT = T // P
NT = B * TT
HG = 4
G = NH // HG
SLOT = 32
NE, CAP, HID = 8, 160, 512
HC = HID // P
N = B * T
SLOTS = NE * CAP
NPB = 4
LAG = 3
QUAD = 4
LNS = 3 * TT
HALF = CAP // 2
NEG = -1.0e30
SM_SCALE = float(DH) ** -0.5
EPS = 1e-5
MAGIC = 1597463007.0
LAST = 2 * N


class Steps:

    def __init__(self, eng, sem, base):
        self.eng, self.sem, self.value = eng, sem, base

    def did(self, ins):
        ins.then_inc(self.sem, 1)
        self.value = self.value + 1

    def skip(self, n):
        self.eng.sem_inc(self.sem, n)
        self.value = self.value + n

    def wait(self, plain=None):
        self.eng.wait_ge(self.sem, self.value)
        if plain is not None:
            settle(self.eng, plain)


def rsqrt(nc, st, var, y, h, t, between=None):
    v = nc.vector
    other = between or (lambda k: None)
    st.did(v.tensor_scalar(h, var, EPS, None, ALU.add))
    other(0)
    st.wait()
    st.did(v.tensor_scalar(t.bitcast(I32), h.bitcast(I32), 1, None, ALU.arith_shift_right))
    other(1)
    st.wait()
    st.did(v.tensor_scalar(y.bitcast(I32), t.bitcast(I32), -1.0, MAGIC, ALU.mult, ALU.add))
    other(2)
    for k in range(3):
        st.wait()
        st.did(v.tensor_tensor(t, y, y, ALU.mult))
        other(3 * k + 3)
        st.wait()
        st.did(v.scalar_tensor_tensor(t, t, -0.5, h, ALU.mult, ALU.mult))
        other(3 * k + 4)
        st.wait()
        st.did(v.scalar_tensor_tensor(y, t, 1.5, y, ALU.add, ALU.mult))
        other(3 * k + 5)
    st.wait()


RSQRT_STEPS = 12
ROUTE = 26
CREDIT = 1


def settle(eng, passed):
    eng.sem_inc(passed, 1)


def wait(eng, sem, value):
    if isinstance(value, int) and value <= 0:
        return
    eng.wait_ge(sem, value)


def layer_kernel(nc, x, w_qkvo, bo, cos, sin, masks, eye, router_w, router_b, w1, b1, w2, b2,
                 ow1, ob1, ow2, ob2, tri, rank_table, tokens, idx_init, out, slot_tok, x1_dram):
    ctx = ExitStack()
    with ctx:
        phase1 = ExitStack()

        def sb(name, shape, dt=F32, held=ctx):
            return held.enter_context(nc.sbuf_tensor(name, shape, dt))

        def pb(name, shape, dt=F32):
            return ctx.enter_context(nc.psum_tensor(name, shape, dt))

        def sem(name):
            return ctx.enter_context(nc.semaphore(name))

        x_sb = sb("x_sb", [P, N])
        xn2T = sb("xn2T", [P, N])
        logits = sb("logits", [P, NT, NE])
        w_sb = sb("w_sb", [P, 4 * D])
        bo_sb = sb("bo_sb", [P, D])
        cos_sb = sb("cos_sb", [P, TT, DH])
        sin_sb = sb("sin_sb", [P, TT, DH])
        mask_f = sb("mask_f", [P, 2, 4 * P])
        mask_sb = sb("mask_sb", [P, 2, 4 * P], BF16)
        eye_f = sb("eye_f", [P, P])
        eye_r = sb("eye_r", [P, P], F32R)
        eye_b = sb("eye_b", [P, P], BF16)
        rw_sb = sb("rw_sb", [P, NE])
        rb_sb = sb("rb_sb", [P, NE])

        ow1_sb = sb("ow1_sb", [P, HID])
        ow2_sb = sb("ow2_sb", [P, HC, D])
        ob1_sb = sb("ob1_sb", [P, HC])
        ob2_sb = sb("ob2_sb", [P, D])
        b1_sb = sb("b1_sb", [P, NE, HC])
        b2_sb = sb("b2_sb", [P, NE, D])
        tri_f = sb("tri_f", [P, P])
        rank_c = sb("rank_c", [P, 2, NE])
        tok_id = sb("tok_id", [P, NT], I32)

        k_diag = [sb(f"k_diag{i}", [P, G, HG, T], F32R, held=phase1) for i in range(2)]
        xn = sb("xn", [P, TT, D], held=phase1)
        ln_st = sb("ln_st", [P, LNS, 6], held=phase1)
        ln_mv = sb("ln_mv", [P, LNS, 2], held=phase1)
        ln_y = sb("ln_y", [P, LNS], held=phase1)
        ln_b = sb("ln_b", [P, LNS], held=phase1)
        ln_h = sb("ln_h", [P, LNS], held=phase1)
        ln_t = sb("ln_t", [P, LNS], held=phase1)
        xnT = sb("xnT", [P, T], held=phase1)
        rope_c = sb("rope_c", [P, TT, 2 * NH, DH], held=phase1)
        rope_s = sb("rope_s", [P, TT, 2 * NH, DH], held=phase1)
        rope = sb("rope", [P, TT, 2 * NH, DH], held=phase1)
        v_raw = sb("v_raw", [P, TT, NH, DH], held=phase1)
        aug = [sb(f"aug{i}", [P, TT, 2 * NH, SLOT], F32R, held=phase1) for i in range(2)]
        ones_f = sb("ones_f", [P, 2 * TT * NH], held=phase1)
        qT_max = sb("qT_max", [P, G, T], F32R, held=phase1)
        qT = [sb(f"qT{i}", [P, G, T], F32R, held=phase1) for i in range(2)]
        neg_max = sb("neg_max", [P, TT, NH], held=phase1)
        v_aug = [sb(f"v_aug{i}", [P, TT, NH, SLOT], held=phase1) for i in range(2)]
        probs = [sb(f"probs{i}", [P, 3 * P], held=phase1) for i in range(NPB)]
        oT = sb("oT", [P, G, T], held=phase1)
        rden = sb("rden", [P, NH], held=phase1)
        o_tok = sb("o_tok", [P, TT, NH, DH], held=phase1)
        o_tokT = sb("o_tokT", [P, T], held=phase1)
        at = sb("at", [P, TT, D], held=phase1)
        xn2 = sb("xn2", [P, TT, D], held=phase1)
        xn2T_now = sb("xn2T_now", [P, T], held=phase1)
        phase1.close()

        hid = [sb(f"hid{i}", [P, HC, QUAD * P]) for i in range(2)]
        tri_b = sb("tri_b", [P, P], BF16)
        ones_b = sb("ones_b", [P, P], BF16)
        best = sb("best", [P, NT])
        pick = sb("pick", [P, NT, NE])
        hot = sb("hot", [P, NT, NE])
        hot_b = sb("hot_b", [P, NT, NE], BF16)
        total = sb("total", [P, NE, NT])
        upto = sb("upto", [P, NE, NT])
        zeros = sb("zeros", [P, NT])
        slot_f = sb("slot_f", [P, NT])
        slot_i = sb("slot_i", [P, NT], I32)
        LOT = 8
        lot_slot = [sb(f"lot_slot{i}", [P, LOT], I32) for i in range(2)]
        lot_tok = [sb(f"lot_tok{i}", [P, LOT], I32) for i in range(2)]
        y_sb = sb("y_sb", [P, 2 * QUAD, D])
        y_st = sb("y_st", [P, 2 * QUAD, 6])
        y_mv = sb("y_mv", [P, 2 * QUAD, 2])
        y_y = sb("y_y", [P, 2 * QUAD])
        y_h = sb("y_h", [P, 2 * QUAD])
        y_t = sb("y_t", [P, 2 * QUAD])
        fin = [sb(f"fin{i}", [P, QUAD, D]) for i in range(2)]
        PARTS = ((0, 2), (2, 4), (4, 6), (6, 8))
        KT = NE * 2
        slot_idx = sb("slot_idx", [HALF, KT], I32)
        xg = sb("xg", [HALF, KT, D])
        g_st = sb("g_st", [HALF, KT, 6])
        g_mv = sb("g_mv", [HALF, KT, 2])
        g_y = sb("g_y", [HALF, KT])
        g_h = sb("g_h", [HALF, KT])
        g_t = sb("g_t", [HALF, KT])
        g_b = sb("g_b", [HALF, KT])
        r_st = sb("r_st", [HALF, KT, 6])
        r_mv = sb("r_mv", [HALF, KT, 2])
        r_y = sb("r_y", [HALF, KT])
        r_h = sb("r_h", [HALF, KT])
        r_t = sb("r_t", [HALF, KT])
        r_b = sb("r_b", [HALF, KT])
        xgn = sb("xgn", [HALF, KT, D])
        xgT = sb("xgT", [P, SLOTS])
        NW = 4
        w1_sb = [sb(f"w1_sb{i}", [P, HID]) for i in range(NW)]
        w2_sb = sb("w2_sb", [P, NE, HC, D])
        hid_e = [sb(f"hid_e{i}", [P, HC, CAP]) for i in range(2)]
        y_e = sb("y_e", [HALF, KT, D])

        ps_w = pb("ps_w", [P, 2, 512])
        ps_a = [pb(f"ps_a{i}", [P, 512]) for i in range(2)]
        ps_s = [pb(f"ps_s{i}", [P, 512]) for i in range(2)]
        ps_o = pb("ps_o", [P, 512])
        ps_b = pb("ps_b", [P, 512])

        consts_in = sem("consts_in")
        x_first = sem("x_first")
        x_rest = sem("x_rest")
        consts_ready = sem("consts_ready")
        pads_ready = sem("pads_ready")
        half_ready = sem("half_ready")
        ones_ready = sem("ones_ready")
        norms_step = sem("norms_step")
        xstat_ready = sem("xstat_ready")
        xn_ready = sem("xn_ready")
        xn2_ready = sem("xn2_ready")
        xt_done = sem("xt_done")
        xnT_ready = sem("xnT_ready")
        qkv_done = sem("qkv_done")
        rope_parts = sem("rope_parts")
        rope_ready = sem("rope_ready")
        vraw_ready = sem("vraw_ready")
        hi_ready = sem("hi_ready")
        hi_copied = sem("hi_copied")
        aug_ready = sem("aug_ready")
        kt_done = sem("kt_done")
        kdiag_act = sem("kdiag_act")
        kdiag_dve = sem("kdiag_dve")
        qt_done = sem("qt_done")
        qt_shifted = sem("qt_shifted")
        qtmax_ready = sem("qtmax_ready")
        sa_done = sem("sa_done")
        max_done = sem("max_done")
        shift_step = sem("shift_step")
        qT_ready = sem("qT_ready")
        vaug_ready = sem("vaug_ready")
        s_done = sem("s_done")
        exp_done = sem("exp_done")
        sel_done = sem("sel_done")
        pv_done = sem("pv_done")
        oT_ready = sem("oT_ready")
        otok_psum = sem("otok_psum")
        norm_step = sem("norm_step")
        otokT_done = sem("otokT_done")
        otokT_ready = sem("otokT_ready")
        y_done = sem("y_done")
        at_ready = sem("at_ready")
        x1_ready = sem("x1_ready")
        xn2t_done = sem("xn2t_done")
        xn2T_ready = sem("xn2T_ready")
        xn2T_kept = sem("xn2T_kept")
        lg_psum = sem("lg_psum")
        lg_ready = sem("lg_ready")
        dve_passed = sem("dve_passed")
        pool_passed = sem("pool_passed")
        late_in = sem("late_in")
        table_init = sem("table_init")
        x1_stored = sem("x1_stored")
        route_step = sem("route_step")
        rank_psum = sem("rank_psum")
        lot_ready = sem("lot_ready")
        scattered = [sem(f"scattered{i}") for i in range(2)]
        h_done = sem("h_done")
        hid_ready = sem("hid_ready")
        yov_done = sem("yov_done")
        over_step = sem("over_step")
        last_step = sem("last_step")
        out_stored = [sem(f"out_stored{i}") for i in range(2)]
        idx_in = sem("idx_in")
        xg_clear = sem("xg_clear")
        gathered = [sem(f"gathered{i}") for i in range(NE * 2 // QUAD)]
        w1_in = [sem(f"w1_in{i}") for i in range(NW)]
        w2_in = sem("w2_in")
        gnorm_step = sem("gnorm_step")
        xgn_ready = sem("xgn_ready")
        gT_psum = sem("gT_psum")
        xgT_ready = sem("xgT_ready")
        he_done = sem("he_done")
        hid_e_ready = sem("hid_e_ready")
        ye_done = sem("ye_done")
        ye_read = sem("ye_read")
        res_step = sem("res_step")
        y_scaled = sem("y_scaled")
        res_ready = sem("res_ready")
        res_stored = sem("res_stored")

        NORMS = 2 * LNS + RSQRT_STEPS + TT
        STEPS2 = NT // QUAD
        OVER = 1 + 2 * QUAD + RSQRT_STEPS + QUAD + 1
        LAST_STEPS = 2 + 2 * 2 * QUAD + RSQRT_STEPS + 2 * QUAD + 2
        GNORM = 2 * NE + RSQRT_STEPS + 1
        RES_STEPS = [2 * end_e + (part + 1) * (RSQRT_STEPS + 1) for part, (_, end_e) in enumerate(PARTS)]
        YE = 3
        h_bank = [ps_w[:, 0], ps_w[:, 1], ps_a[0][:], ps_a[1][:]]
        y_bank = [ps_s[0][:], ps_s[1][:]]
        g_bank = [h_bank[0], h_bank[1], ps_o[:], ps_b[:]]
        block = ctx.enter_context(nc.Block())

        @block.sync
        def _(sp):
            xt = x.rearrange("(n p) d -> p n d", p=P)
            xs = x_sb[:].rearrange("p (n d) -> p n d", d=D)
            first = 3 * TT
            sp.dma_start(xs[:, 0:first, :], xt[:, 0:first, :]).then_inc(x_first, 16)
            for dst, src in ((w_sb[:], w_qkvo), (bo_sb[:], bo), (cos_sb[:], cos), (sin_sb[:], sin),
                             (mask_f[:], masks), (eye_f[:], eye), (rw_sb[:], router_w),
                             (rb_sb[:], router_b)):
                sp.dma_start(dst, src).then_inc(consts_in, 16)
            sp.dma_start(xs[:, first:, :], xt[:, first:, :]).then_inc(x_rest, 16)
            sp.dma_start(slot_tok, idx_init).then_inc(table_init, 16)
            for dst, src in ((ow1_sb[:], ow1), (ow2_sb[:], ow2.rearrange("(m p) d -> p m d", p=P)),
                             (ob1_sb[:], ob1), (ob2_sb[:], ob2), (b1_sb[:], b1), (b2_sb[:], b2),
                             (tri_f[:], tri), (rank_c[:], rank_table), (tok_id[:], tokens)):
                sp.dma_start(dst, src).then_inc(late_in, 16)
            sp.wait_ge(x1_ready, B)
            sp.dma_start(x1_dram.rearrange("(n p) d -> p n d", p=P), xs).then_inc(x1_stored, 16)
            sp.wait_ge(lg_ready, B + CREDIT)
            sp.wait_ge(xn2T_kept, B + CREDIT)
            sp.dma_start(w2_sb[:], w2.rearrange("e (m p) d -> p e m d", p=P)).then_inc(w2_in, 16)
            for e in range(NW):
                sp.dma_start(w1_sb[e][:], w1[e]).then_inc(w1_in[e], 16)
            ot = out.rearrange("(n p) d -> p n d", p=P)
            with sp.Fori(0, STEPS2 // 2 - 1) as k:
                for par in range(2):
                    i = k * 2 + par
                    sp.wait_ge(over_step, OVER * (i + 1) + CREDIT)
                    sp.dma_start(ot[:, bass.ds(i * QUAD, QUAD), :], fin[par][:])\
                        .then_inc(out_stored[par], 16)
            for e in range(NW, NE):
                sp.wait_ge(he_done, HC * (e - NW + 1))
                sp.dma_start(w1_sb[e - NW][:], w1[e]).then_inc(w1_in[e - NW], 16)
            for par in range(2):
                i = STEPS2 - 2 + par
                sp.wait_ge(last_step, LAST_STEPS - 1 + par)
                sp.dma_start(ot[:, i * QUAD:(i + 1) * QUAD, :], fin[par][:]).then_inc(out_stored[par], 16)

        @block.vector
        def _(dve):
            v = nc.vector
            v.memset(k_diag[1][:, 0:2].bitcast(F32), 0.0).then_inc(half_ready, 1)

            def constants():
                dve.wait_ge(consts_in, 16 * 8)
                v.tensor_copy(eye_r[:], eye_f[:])
                v.tensor_copy(eye_b[:], eye_f[:])
                v.tensor_copy(mask_sb[:], mask_f[:]).then_inc(consts_ready, 1)

            def rotary(b):
                dve.wait_ge(qkv_done, TT * (b + 1))
                wait(dve, rope_ready, b)
                qk = ps_w[:, :, 0:2 * D].rearrange("p t (h d) -> p t h d", d=DH)
                full = [P, TT, 2 * NH, DH]
                half = [P, TT, 2 * NH, DH // 2]
                h = DH // 2
                v.tensor_tensor(rope_c[:], qk, cos_sb[:].unsqueeze(2).broadcast_to(full), ALU.mult)
                v.tensor_tensor(rope_s[:, :, :, 0:h], qk[:, :, :, h:],
                                sin_sb[:, :, 0:h].unsqueeze(2).broadcast_to(half), ALU.mult)
                v.tensor_tensor(rope_s[:, :, :, h:], qk[:, :, :, 0:h],
                                sin_sb[:, :, h:].unsqueeze(2).broadcast_to(half),
                                ALU.mult).then_inc(rope_parts, 1)

            def spread_k(b, par, half, cs):
                dve.wait_ge(kt_done, 2 * b + half + 1)
                for c in cs:
                    q = slice(32 * c, 32 * c + 32)
                    last = v.tensor_copy(k_diag[par][q, 2 * half:2 * half + 2, c, :],
                                         ps_w[q, half].rearrange("p (g t) -> p g t", t=T))
                last.then_inc(kdiag_dve, 1)

            def row_max(b, u):
                g, k = divmod(u, 3)
                dve.wait_ge(sa_done, 12 * b + u + 1)
                if k == 0:
                    o = neg_max[:, 0, HG * g:HG * g + HG]
                    i = ps_a[u % 2][:].rearrange("p (h k) -> p h k", h=HG)
                else:
                    o = neg_max[:, 1, HG * g + 2 * (k - 1):HG * g + 2 * k]
                    i = ps_a[u % 2][:].rearrange("p (h k) -> p h k", h=2)
                v.tensor_reduce(o, i, AX.X, ALU.max, negate=True).then_inc(max_done, 1)

            def shift(b, par, half):
                dve.wait_ge(max_done, 12 * b + 6 * half + 6)
                h = slice(NH // 2 * half, NH // 2 * (half + 1))
                st = Steps(dve, shift_step, 4 * b + 2 * half)
                st.did(v.tensor_copy(aug[par][:, :, h, 24], neg_max[:, :, h]))
                st.wait()
                st.did(v.tensor_tensor(aug[par][:, :, h, 25], neg_max[:, :, h],
                                       aug[par][:, :, h, 24].bitcast(F32), ALU.subtract))

            def divide(b, t):
                dve.wait_ge(otok_psum, 2 * b + t + 1)
                st = Steps(dve, norm_step, 4 * b + 2 * t)
                o = ps_b[:].rearrange("p (h s) -> p h s", s=SLOT)
                if t == 0:
                    wait(dve, otokT_done, b)
                st.did(v.reciprocal(rden[:], o[:, :, DH]))
                st.wait()
                st.did(v.tensor_tensor(o_tok[:, t], o[:, :, 0:DH],
                                       rden[:].unsqueeze(2).broadcast_to([P, NH, DH]), ALU.mult))

            def attn_out(b):
                dve.wait_ge(y_done, b + 1)
                wait(dve, x1_ready, b)
                v.tensor_tensor(at[:], ps_b[:, 0:T].rearrange("p (t d) -> p t d", t=TT),
                                bo_sb[:].unsqueeze(1).broadcast_to([P, TT, D]), ALU.add)\
                    .then_inc(at_ready, 1)

            def norms(n, has, between):
                tile = lambda b: lambda t: x_sb[:, bass.ds(b * T + t * D, D)]
                parts = [(0, n + 3, tile(n + 3), xn), (1, n - 2, lambda t: at[:, t], at),
                         (2, n - 3, tile(n - 3), xn2)]
                parts = [p for p in parts if has(p[1])]
                if not parts:
                    for k in range(RSQRT_STEPS + 5):
                        between(k)
                    return
                st = Steps(dve, norms_step, (n + 3) * NORMS)
                for q, b, src, dst in parts:
                    if q == 0:
                        dve.wait_ge(x_first if isinstance(n, int) and n < 0 else x_rest, 16)
                    else:
                        dve.wait_ge(at_ready if q == 1 else x1_ready, b + 1)
                        settle(dve, dve_passed)
                    for t in range(TT):
                        st.did(v.bn_stats(out=ln_st[:, q * TT + t], in_=src(t)))
                between(0)
                st.wait(dve_passed)
                for q, b, src, dst in parts:
                    for t in range(TT):
                        st.did(v.bn_aggr(out=ln_mv[:, q * TT + t], in_=ln_st[:, q * TT + t]))
                between(1)
                if len(parts) < 3:
                    st.skip(2 * TT * (3 - len(parts)))
                st.wait()
                cs = slice(parts[0][0] * TT, parts[-1][0] * TT + TT)
                if has(n + 3):
                    wait(dve, xn_ready, n + 3)
                rsqrt(nc, st, ln_mv[:, cs, 1], ln_y[:, cs], ln_h[:, cs], ln_t[:, cs],
                      lambda k: between(k + 2))
                for q in range(3):
                    for _, b, src, dst in [p for p in parts if p[0] == q]:
                        if q == 0:
                            xc = slice(0, TT)
                            v.scalar_tensor_tensor(ln_b[:, xc], ln_mv[:, xc, 0], -1.0, ln_y[:, xc],
                                                   ALU.mult, ALU.mult).then_inc(xstat_ready, 1)
                            continue
                        if q == 2:
                            wait(dve, xn2t_done, b + CREDIT)
                        for t in range(TT):
                            c = q * TT + t
                            ins = v.tensor_scalar(dst[:, t], src(t), ln_mv[:, c, 0:1],
                                                  ln_y[:, c:c + 1], ALU.subtract, ALU.mult)
                            if q == 1:
                                st.did(ins)
                        if q == 2:
                            ins.then_inc(xn2_ready, 1)
                    between(RSQRT_STEPS + 2 + q)
                if has(n - 2):
                    st.wait()
                    row = x_sb[:, bass.ds((n - 2) * T, T)]
                    v.tensor_tensor(row, row, at[:].rearrange("p t d -> p (t d)"), ALU.add)\
                        .then_inc(x1_ready, 1)
                else:
                    st.skip(TT)

            def logits_out(b):
                dve.wait_ge(lg_psum, b + 1)
                v.tensor_tensor(logits[:, bass.ds(b * TT, TT), :],
                                ps_b[:, 0:TT * NE].rearrange("p (t e) -> p t e", e=NE),
                                rb_sb[:].unsqueeze(1).broadcast_to([P, TT, NE]),
                                ALU.add).then_inc(lg_ready, 1)

            def step(n, par, has):
                f1, f2, b2, b4 = has(n + 2), has(n + 1), has(n - 1), has(n - 3)

                def between(k):
                    if f2 and k == 1:
                        row_max(n + 1, 0)
                    if f2 and k == 2:
                        spread_k(n + 1, 1 - par, 1, (3,))
                    if f2 and k == 3:
                        row_max(n + 1, 1)
                    if f2 and k == 4:
                        row_max(n + 1, 2)
                    if b2 and k == 5:
                        divide(n - 1, 0)
                    if f2 and k == 8:
                        row_max(n + 1, 3)
                    if f2 and k == 9:
                        row_max(n + 1, 4)
                    if b2 and k == 10:
                        divide(n - 1, 1)
                    if f2 and k == 11:
                        row_max(n + 1, 5)
                    if f1 and k == 12:
                        rotary(n + 2)
                    if f2 and k == 13:
                        row_max(n + 1, 6)
                    if f2 and k == 14:
                        row_max(n + 1, 7)
                        shift(n + 1, 1 - par, 0)
                        row_max(n + 1, 8)
                    if f2 and k == 15:
                        row_max(n + 1, 9)

                norms(n, has, between)
                if has(n + 3) and not has(n + 2):
                    constants()
                if b2:
                    attn_out(n - 1)
                if f2:
                    row_max(n + 1, 10)
                    row_max(n + 1, 11)
                if f1:
                    spread_k(n + 2, par, 0, (2, 3))
                if f2:
                    shift(n + 1, 1 - par, 1)
                if b4:
                    logits_out(n - 3)

            dve.sem_inc(lg_ready, CREDIT)
            steady(dve, step)

            dve.wait_ge(late_in, 16 * 9)
            dve.wait_ge(lg_ready, B + CREDIT)
            st = Steps(dve, route_step, 0)
            st.did(v.memset(ones_b[:], 1.0))
            st.did(v.memset(zeros[:], 0.0))
            st.did(v.tensor_copy(tri_b[:], tri_f[:]))
            per_tile = lambda a: a.unsqueeze(2).broadcast_to([P, NT, NE])
            per_expert = lambda a: a.unsqueeze(1).broadcast_to([P, NT, NE])
            st.did(v.tensor_reduce(best[:], logits[:], AX.X, ALU.max))
            st.wait()
            st.did(v.tensor_tensor(pick[:], logits[:], per_tile(best[:]), ALU.is_ge))
            st.wait()
            st.did(v.tensor_tensor(pick[:], pick[:], per_expert(rank_c[:, 0]), ALU.mult))
            st.wait()
            st.did(v.tensor_reduce(best[:], pick[:], AX.X, ALU.max))
            st.wait()
            st.did(v.tensor_tensor(hot[:], pick[:], per_tile(best[:]), ALU.is_equal))
            st.wait()
            st.did(v.tensor_copy(hot_b[:], hot[:]))
            dve.wait_ge(rank_psum, 1)
            st.did(v.tensor_copy(total[:], ps_b[:].rearrange("p (n e) -> p e n", e=NE)))
            st.wait()
            for e in range(NE):
                st.did(v.tensor_tensor_scan(upto[:, e], total[:, e], zeros[:], 0.0, ALU.add, ALU.add))
            st.wait()
            st.did(v.tensor_tensor(upto[:], upto[:], total[:], ALU.subtract))
            st.wait()
            st.did(v.tensor_tensor(pick[:], ps_o[:].rearrange("p (n e) -> p n e", e=NE),
                                   upto[:].rearrange("p e n -> p n e"), ALU.add))
            st.wait()
            lg = logits[:]
            st.did(v.tensor_scalar(lg, pick[:], float(CAP) + 0.5, 1.0e5, ALU.is_gt, ALU.mult))
            st.wait()
            st.did(v.tensor_tensor(pick[:], pick[:], lg, ALU.add))
            st.wait()
            st.did(v.tensor_tensor(pick[:], pick[:], per_expert(rank_c[:, 1]), ALU.add))
            st.wait()
            st.did(v.tensor_tensor(pick[:], pick[:], hot[:], ALU.mult))
            st.wait()
            st.did(v.tensor_reduce(slot_f[:], pick[:], AX.X, ALU.add))
            st.wait()
            st.did(v.tensor_copy(slot_i[:], slot_f[:]))
            assert st.value == ROUTE

            def norm_stats(st, src, stats, mv, ks):
                for k in ks:
                    st.did(v.bn_stats(out=stats[:, k], in_=src[:, k]))
                st.wait(dve_passed)
                for k in ks:
                    st.did(v.bn_aggr(out=mv[:, k], in_=stats[:, k]))
                st.wait()

            def norm_scale(st, src, dst, mv, y, ks):
                for k in ks:
                    st.did(v.tensor_scalar(dst[:, k], src[:, k], mv[:, k, 0:1], y[:, k:k + 1],
                                           ALU.subtract, ALU.mult))

            def over_read(st, i, par):
                dve.wait_ge(yov_done, i + 3)
                st.did(v.tensor_tensor(y_sb[:, par * QUAD:(par + 1) * QUAD],
                                       y_bank[par].rearrange("p (n d) -> p n d", d=D),
                                       ob2_sb[:].unsqueeze(1).broadcast_to([P, QUAD, D]), ALU.add))

            def over_add(st, k2, par):
                i = k2 * 2 + par
                dve.wait_ge(out_stored[par], k2 * 16 + 16)
                st.did(v.tensor_tensor(fin[par][:].rearrange("p n d -> p (n d)"),
                                       x_sb[:, bass.ds(i * QUAD * D, QUAD * D)],
                                       y_sb[:, par * QUAD:(par + 1) * QUAD].rearrange("p n d -> p (n d)"),
                                       ALU.add))

            dve.sem_inc(over_step, CREDIT)
            for par in range(2):
                dve.sem_inc(out_stored[par], 16)
            def over_out(k2, par, while_read=None):
                i = k2 * 2 + par
                ks = range(par * QUAD, (par + 1) * QUAD)
                cs = slice(ks[0], ks[-1] + 1)
                dve.wait_ge(over_step, OVER * i + CREDIT)
                st = Steps(dve, over_step, OVER * i + CREDIT)
                over_read(st, i, par)
                if while_read is not None:
                    while_read()
                st.wait(dve_passed)
                norm_stats(st, y_sb, y_st, y_mv, ks)
                rsqrt(nc, st, y_mv[:, cs, 1], y_y[:, cs], y_h[:, cs], y_t[:, cs])
                norm_scale(st, y_sb, y_sb, y_mv, y_y, ks)
                st.wait()
                over_add(st, k2, par)

            with dve.Fori(0, STEPS2 // 2 - 2) as k2:
                for par in range(2):
                    over_out(k2, par)

            def tokens_norm(half):
                ks = range(half * NE, (half + 1) * NE)
                cs = slice(ks[0], ks[-1] + 1)
                for lot in range(ks[0] // QUAD, ks[-1] // QUAD + 1):
                    dve.wait_ge(gathered[lot], 16 * QUAD)
                st = Steps(dve, gnorm_step, half * GNORM)
                norm_stats(st, xg, g_st, g_mv, ks)
                rsqrt(nc, st, g_mv[:, cs, 1], g_y[:, cs], g_h[:, cs], g_t[:, cs])
                st.did(v.scalar_tensor_tensor(g_b[:, cs], g_mv[:, cs, 0], -1.0, g_y[:, cs],
                                              ALU.mult, ALU.mult))
                assert st.value == (half + 1) * GNORM

            def expert_read(e):
                dve.wait_ge(ye_done, e + 3)
                st = Steps(dve, ye_read, (e + 2) * YE)
                st.did(v.tensor_tensor(y_e[:, 2 * e:2 * e + 2, :],
                                       y_bank[e % 2][0:HALF, 0:2 * D].rearrange("p (n d) -> p n d", d=D),
                                       b2_sb[0:HALF, e:e + 1, :].broadcast_to([HALF, 2, D]),
                                       ALU.add))
                st.wait(dve_passed)
                for t in range(2):
                    st.did(v.bn_stats(out=r_st[:, 2 * e + t], in_=y_e[:, 2 * e + t]))

            def experts_norm(part, between=None):
                first_e, end_e = PARTS[part]
                dve.wait_ge(ye_read, (end_e + 2) * YE)
                ks = range(2 * first_e, 2 * end_e)
                cs = slice(ks[0], ks[-1] + 1)
                st = Steps(dve, res_step, first_e * 2 + part * (RSQRT_STEPS + 1))
                for k in ks:
                    st.did(v.bn_aggr(out=r_mv[:, k], in_=r_st[:, k]))
                st.wait()
                rsqrt(nc, st, r_mv[:, cs, 1], r_y[:, cs], r_h[:, cs], r_t[:, cs], between)
                st.did(v.scalar_tensor_tensor(r_b[:, cs], r_mv[:, cs, 0], -1.0, r_y[:, cs],
                                              ALU.mult, ALU.mult))
                assert st.value == RES_STEPS[part]

            def experts_add(part):
                cs = slice(2 * PARTS[part][0], 2 * PARTS[part][1])
                dve.wait_ge(y_scaled, cs.stop)
                v.tensor_tensor(y_e[:, cs], y_e[:, cs], xg[:, cs], ALU.add).then_inc(res_ready, 1)

            over_out(STEPS2 // 2 - 2, 0)
            over_out(STEPS2 // 2 - 2, 1, lambda: tokens_norm(0))
            st = Steps(dve, last_step, 0)
            for par in range(2):
                dve.wait_ge(over_step, OVER * (STEPS2 - 3 + par) + CREDIT)
                over_read(st, STEPS2 - 2 + par, par)
            dve.sem_inc(ye_read, 2 * YE)
            tokens_norm(1)
            for e in range(2):
                expert_read(e)
            st.wait(dve_passed)
            experts_norm(0, lambda k: st.did(v.bn_stats(out=y_st[:, k], in_=y_sb[:, k]))
                         if k < 2 * QUAD else None)
            expert_read(2)
            st.wait(dve_passed)
            for k in range(2 * QUAD):
                st.did(v.bn_aggr(out=y_mv[:, k], in_=y_st[:, k]))
            expert_read(3)
            st.wait()
            rsqrt(nc, st, y_mv[:, :, 1], y_y[:], y_h[:], y_t[:])
            norm_scale(st, y_sb, y_sb, y_mv, y_y, range(2 * QUAD))
            st.wait()
            for par in range(2):
                over_add(st, STEPS2 // 2 - 1, par)
            assert st.value == LAST_STEPS
            expert_read(4)
            experts_add(0)
            experts_norm(1, lambda k: expert_read(5) if k == 6 else None)
            experts_norm(2, lambda k: experts_add(1) if k == 5 else expert_read(6) if k == 8 else None)
            expert_read(7)
            experts_norm(3, lambda k: experts_add(2) if k == 7 else None)
            experts_add(3)

        @block.gpsimd
        def _(pool):
            gp = nc.gpsimd
            zero = pool.to_reg(0.0)
            for i in range(2):
                gp.memset(aug[i][:].bitcast(F32), 0.0).then_inc(pads_ready, 1)
                gp.memset(v_aug[i][:], 0.0).then_inc(pads_ready, 1)
                gp.memset(k_diag[i][:, 2 * i:].bitcast(F32), 0.0).then_inc(pads_ready, 1)
                if i == 0:
                    gp.memset(ones_f[:], 1.0).then_inc(pads_ready, 1)
                else:
                    pool.wait_ge(half_ready, 1)
                pool.wait_ge(pads_ready, 4 + 3 * i)
                gp.tensor_copy(aug[i][:, :, NH:, 24:26],
                               ones_f[:].rearrange("p (t h s) -> p t h s", t=TT, s=2))
                gp.memset(v_aug[i][:, :, :, DH:DH + 1], 1.0).then_inc(ones_ready, 1)

            def sum_rope(b):
                pool.wait_ge(rope_parts, b + 1)
                wait(pool, hi_copied, b)
                wait(pool, aug_ready, b)
                gp.tensor_tensor(rope[:], rope_c[:], rope_s[:], ALU.add).then_inc(rope_ready, 1)

            def low_parts(b, par):
                pool.wait_ge(hi_ready, b + 1)
                a = aug[par]
                gp.tensor_tensor(a[:, :, 0:NH, 16:24], rope[:, :, 0:NH],
                                 a[:, :, 0:NH, 0:8].bitcast(F32), ALU.subtract)
                gp.tensor_tensor(a[:, :, NH:, 8:16], rope[:, :, NH:],
                                 a[:, :, NH:, 0:8].bitcast(F32), ALU.subtract)
                gp.memset(a[:, :, 0:NH, 24:26].bitcast(F32), 0.0).then_inc(aug_ready, 1)

            def keep_v(b, par):
                pool.wait_ge(vraw_ready, b + 1)
                wait(pool, pv_done, NH * (b - 1))
                settle(pool, pool_passed)
                gp.tensor_copy(v_aug[par][:, :, :, 0:DH], v_raw[:]).then_inc(vaug_ready, 1)

            def causal(b, j):
                J = NH * b + j
                pool.wait_ge(exp_done, J + 1)
                settle(pool, pool_passed)
                pr = probs[j % NPB]
                d = pr[:, 0:2 * P].rearrange("p (a q) -> p a q", a=2)
                gp.affine_select(out=d, in_=d, compare_op=ALU.is_ge, fill=zero, base=0,
                                 pattern=[[0, 2], [1, P]], channel_multiplier=-1)
                e = pr[:, 2 * P:3 * P]
                gp.affine_select(out=e, in_=e, compare_op=ALU.is_ge, fill=zero, base=-1,
                                 pattern=[[-1, P]], channel_multiplier=1).then_inc(sel_done, 1)

            def keep_xn2T(b):
                pool.wait_ge(xn2T_ready, b + 1)
                settle(pool, pool_passed)
                gp.tensor_copy(xn2T[:, bass.ds(b * T, T)], xn2T_now[:]).then_inc(xn2T_kept, 1)

            def step(n, par, has):
                f1, f2, b4 = has(n + 2), has(n + 1), has(n - 3)
                for j in range(NH):
                    if has(n):
                        causal(n, j)
                    if f2 and j == 3:
                        keep_v(n + 1, 1 - par)
                    if f1 and j == 7:
                        sum_rope(n + 2)
                    if f1 and j == 9:
                        low_parts(n + 2, par)
                if b4:
                    keep_xn2T(n - 3)

            pool.sem_inc(xn2T_kept, CREDIT)
            steady(pool, step)

            pool.wait_ge(lg_ready, B + CREDIT)
            pool.wait_ge(xn2T_kept, B + CREDIT)
            gp.memset(xg[:], 0.0).then_inc(xg_clear, 1)
            pool.wait_ge(table_init, 16)
            pool.wait_ge(route_step, ROUTE)

            def scatter_lot(k2, par):
                i = k2 * 2 + par
                if not isinstance(k2, int):
                    pool.wait_ge(scattered[par], k2 * (16 * LOT))
                    settle(pool, pool_passed)
                gp.tensor_copy(lot_slot[par][:], slot_i[:, bass.ds(i * LOT, LOT)])
                gp.tensor_copy(lot_tok[par][:], tok_id[:, bass.ds(i * LOT, LOT)])\
                    .then_inc(lot_ready, 1)
                pool.wait_ge(lot_ready, i + 1)
                settle(pool, pool_passed)
                for c in range(LOT):
                    gp.indirect_dma_start(
                        out=slot_tok, out_offset=bass.IndirectOffsetOnAxis(ap=lot_slot[par][:, c:c + 1], axis=0),
                        in_=lot_tok[par][:, c:c + 1], in_offset=None, bounds_check=SLOTS - 1,
                        oob_is_err=False).then_inc(scattered[par], 16)

            for par in range(2):
                scatter_lot(0, par)
            with pool.Fori(1, NT // (2 * LOT)) as k2:
                for par in range(2):
                    scatter_lot(k2, par)

            pool.wait_ge(xg_clear, 1)
            for par in range(2):
                pool.wait_ge(scattered[par], 16 * NT // 2)
            gp.dma_start(slot_idx[:], slot_tok.rearrange("(k p) o -> p (k o)", p=HALF),
                         allow_slow_non_contiguous=True).then_inc(idx_in, 16)
            pool.wait_ge(idx_in, 16)
            pool.wait_ge(x1_stored, 16)
            for k in range(KT):
                gp.indirect_dma_start(
                    out=xg[:, k, :], out_offset=None, in_=x1_dram,
                    in_offset=bass.IndirectOffsetOnAxis(ap=slot_idx[:, k:k + 1], axis=0),
                    bounds_check=N - 1, oob_is_err=False).then_inc(gathered[k // QUAD], 16)
            for par in range(2):
                pool.wait_ge(out_stored[par], 16 * STEPS2 // 2 + 16)
            for k in range(KT):
                for part, (first_e, _) in enumerate(PARTS):
                    if k == 2 * first_e:
                        pool.wait_ge(res_ready, part + 1)
                gp.indirect_dma_start(
                    out=out, out_offset=bass.IndirectOffsetOnAxis(ap=slot_idx[:, k:k + 1], axis=0),
                    in_=y_e[:, k, :], in_offset=None, bounds_check=N - 1,
                    oob_is_err=False).then_inc(res_stored, 16)
            pool.wait_ge(res_stored, 16 * KT)

        @block.scalar
        def _(act):
            s = nc.scalar

            def scale_x(b):
                act.wait_ge(xstat_ready, b + 1)
                wait(act, xt_done, b)
                for t in range(TT):
                    last = s.activation(xn[:, t], x_sb[:, bass.ds(b * T + t * D, D)], ACT.Identity,
                                        bias=ln_b[:, t:t + 1], scale=ln_y[:, t:t + 1])
                last.then_inc(xn_ready, 1)

            def evict_xnT(b):
                act.wait_ge(xt_done, b + 1)
                wait(act, qkv_done, TT * b)
                s.copy(xnT[:], ps_w[:, 0, 0:T]).then_inc(xnT_ready, 1)

            def evict_v(b):
                act.wait_ge(rope_parts, b + 1)
                wait(act, vaug_ready, b)
                s.copy(v_raw[:], ps_w[:, :, 2 * D:3 * D].rearrange("p t (h d) -> p t h d", d=DH))\
                    .then_inc(vraw_ready, 1)

            def high_parts(b, par, part):
                a = aug[par]
                if part == 0:
                    if isinstance(b, int) and b < 2:
                        act.wait_ge(ones_ready, b + 1)
                    act.wait_ge(rope_ready, b + 1)
                    s.copy(a[:, :, :, 0:8], rope[:]).then_inc(hi_ready, 1)
                else:
                    s.copy(a[:, :, 0:NH, 8:16], rope[:, :, 0:NH])
                    s.copy(a[:, :, NH:, 16:24], rope[:, :, NH:]).then_inc(hi_copied, 1)

            def spread_k(b, par, half, c, last_c):
                act.wait_ge(kt_done, 2 * b + half + 1)
                q = slice(32 * c, 32 * c + 32)
                last = s.copy(k_diag[par][q, 2 * half:2 * half + 2, c, :],
                              ps_w[q, half].rearrange("p (g t) -> p g t", t=T))
                if c == last_c:
                    last.then_inc(kdiag_act, 1)

            def evict_q(b, half, dst, shifted, ready):
                act.wait_ge(qt_shifted if shifted else qt_done, 2 * b + half + 1)
                s.copy(dst[:, 2 * half:2 * half + 2, :],
                       ps_w[:, half].rearrange("p (g t) -> p g t", t=T)).then_inc(ready, 1)

            def exps(b, j):
                J = NH * b + j
                act.wait_ge(s_done, J + 1)
                wait(act, pv_done, J - NPB + 1)
                s.activation(probs[j % NPB][:], ps_s[j % 2][:, P:4 * P], ACT.Exp,
                             scale=SM_SCALE).then_inc(exp_done, 1)

            def evict_oT(b, g):
                act.wait_ge(pv_done, NH * b + HG * (g + 1))
                s.copy(oT[:, g, :], ps_o[:, 0:T]).then_inc(oT_ready, 1)

            def evict_otokT(b):
                act.wait_ge(otokT_done, b + 1)
                s.copy(o_tokT[:], ps_b[:, 0:T]).then_inc(otokT_ready, 1)

            def evict_xn2T(b):
                act.wait_ge(xn2t_done, b + 1 + CREDIT)
                wait(act, xn2T_kept, b + CREDIT)
                s.copy(xn2T_now[:], ps_b[:, 0:T]).then_inc(xn2T_ready, 1)

            def hidden_relu(i, par):
                act.wait_ge(yov_done, i + 1)
                for m in range(HC):
                    act.wait_ge(h_done, i * HC + m + 1)
                    s.activation(hid[par][:, m, :], h_bank[m], ACT.Relu,
                                 bias=ob1_sb[:, m:m + 1]).then_inc(hid_ready, 1)

            def step(n, par, has):
                f1, f2, b2, b4 = has(n + 2), has(n + 1), has(n - 1), has(n - 3)
                for j in range(NH):
                    if has(n):
                        exps(n, j)
                    if f2 and j == 1:
                        spread_k(n + 1, 1 - par, 1, 0, 2)
                    if b2 and j == 1:
                        evict_oT(n - 1, 3)
                    if f1 and j == 1:
                        evict_xnT(n + 2)
                    if f2 and j == 1:
                        spread_k(n + 1, 1 - par, 1, 1, 2)
                    if f2 and j == 2:
                        spread_k(n + 1, 1 - par, 1, 2, 2)
                    if f2 and j == 3:
                        evict_q(n + 1, 1, qT_max, 0, qtmax_ready)
                    if has(n) and j == 6:
                        evict_oT(n, 0)
                    if f1 and j == 7:
                        evict_v(n + 2)
                    if b2 and j == 8:
                        evict_otokT(n - 1)
                    if f1 and j == 9:
                        high_parts(n + 2, par, 0)
                    if has(n) and j == 9:
                        evict_oT(n, 1)
                    if f2 and j == 10:
                        evict_q(n + 1, 0, qT[1 - par], 1, qT_ready)
                    if f1 and j == 11:
                        high_parts(n + 2, par, 1)
                    if b4 and j == 12:
                        evict_xn2T(n - 3)
                    if f1 and j == 13:
                        spread_k(n + 2, par, 0, 0, 1)
                    if has(n) and j == 13:
                        evict_oT(n, 2)
                    if f1 and j == 13:
                        spread_k(n + 2, par, 0, 1, 1)
                    if f1 and j == 15:
                        evict_q(n + 2, 0, qT_max, 0, qtmax_ready)
                    if f2 and j == 15:
                        evict_q(n + 1, 1, qT[1 - par], 1, qT_ready)
                    if has(n + 3) and j == 15:
                        scale_x(n + 3)
                for i in range(2):
                    if has(n - 1 - i) and not has(n - i):
                        act.wait_ge(late_in, 16 * 9)
                        hidden_relu(i, i)

            steady(act, step)

            with act.Fori(1, STEPS2 // 2) as k2:
                for par in range(2):
                    hidden_relu(k2 * 2 + par, par)

            def evict_tokens(lot):
                act.wait_ge(gT_psum, lot + 1)
                s.copy(xgT[:, lot * QUAD * HALF:(lot + 1) * QUAD * HALF],
                       g_bank[lot][:, 0:QUAD * HALF]).then_inc(xgT_ready, 1)

            def scale_tokens(half):
                act.wait_ge(gnorm_step, (half + 1) * GNORM)
                for k in range(half * NE, (half + 1) * NE):
                    s.activation(xgn[:, k], xg[:, k], ACT.Identity, bias=g_b[:, k:k + 1],
                                 scale=g_y[:, k:k + 1]).then_inc(xgn_ready, 1)

            def expert_relu(e):
                act.wait_ge(ye_done, e + 1)
                for m in range(HC):
                    act.wait_ge(he_done, e * HC + m + 1)
                    s.activation(hid_e[e % 2][:, m, :], h_bank[m][:, 0:CAP], ACT.Relu,
                                 bias=b1_sb[:, e, m:m + 1]).then_inc(hid_e_ready, 1)

            def scale_outputs(part):
                act.wait_ge(res_step, RES_STEPS[part])
                for k in range(2 * PARTS[part][0], 2 * PARTS[part][1]):
                    s.activation(y_e[:, k], y_e[:, k], ACT.Identity, bias=r_b[:, k:k + 1],
                                 scale=r_y[:, k:k + 1]).then_inc(y_scaled, 1)

            scale_tokens(0)
            for half in range(2):
                for lot in range(2 * half, 2 * half + 2):
                    evict_tokens(lot)
                if half == 0:
                    act.sem_inc(hid_e_ready, HC)
                for e in range(half * NE // 2, (half + 1) * NE // 2):
                    expert_relu(e)
                    if e == 1:
                        scale_tokens(1)
                    if e == NE // 2:
                        scale_outputs(0)
            for part in range(1, len(PARTS)):
                scale_outputs(part)

        @block.tensor
        def _(pe):
            mm = nc.tensor.matmul
            tr = nc.tensor.transpose
            w_flat = ps_w[:].rearrange("p a n -> p (a n)")

            def xn_T(b):
                pe.wait_ge(xn_ready, b + 1)
                wait(pe, qtmax_ready, 2 * b - 1)
                for t in range(TT):
                    last = tr(ps_w[:, 0, t * P:(t + 1) * P], xn[:, t], eye_f[:])
                last.then_inc(xt_done, 1)

            def qkv(b, t):
                if t == 0:
                    pe.wait_ge(xnT_ready, b + 1)
                else:
                    wait(pe, qtmax_ready, 2 * b)
                mm(ps_w[:, t, 0:3 * D], xnT[:, t * P:(t + 1) * P], w_sb[:, 0:3 * D])\
                    .then_inc(qkv_done, 1)

            def aug_T(par, first, half):
                for g in (2 * half, 2 * half + 1):
                    for t in range(TT):
                        last = tr(w_flat[:, g * T + t * P:g * T + t * P + P].bitcast(F32R),
                                  aug[par][:, t, first + HG * g:first + HG * g + HG, :]
                                  .rearrange("p h s -> p (h s)"), eye_r[:])
                return last

            def k_T(b, par, half):
                pe.wait_ge(aug_ready, b + 1)
                pe.wait_ge(hi_copied, b + 1)
                wait(pe, qT_ready, 2 * b - 1 + half)
                aug_T(par, NH, half).then_inc(kt_done, 1)

            def q_T(b, par, half, shifted):
                if shifted:
                    pe.wait_ge(shift_step, 4 * b + 2 * half + 2)
                    after = b + 2 if not isinstance(b, int) else min(b + 2, B)
                    pe.wait_ge(rope_parts, after)
                    pe.wait_ge(vraw_ready, after)
                else:
                    pe.wait_ge(kdiag_act, 2 * b + half + 1)
                    pe.wait_ge(kdiag_dve, 2 * b + half + 1)
                aug_T(par, 0, half).then_inc(qt_shifted if shifted else qt_done, 1)

            def max_scores(b, par, u):
                g, k = divmod(u, 3)
                if u in (0, 6):
                    pe.wait_ge(qtmax_ready, 2 * b + 1 + u // 6)
                wait(pe, max_done, 12 * b + u - 1)
                bank = ps_a[u % 2][:]
                if k == 0:
                    keys = k_diag[par][:, g, :, 0:P]
                    q = qT_max[:, g, 0:P]
                else:
                    keys = k_diag[par][:, g, 2 * (k - 1):2 * k, :]
                    q = qT_max[:, g, P:T]
                mm(bank, eye_b[:], mask_sb[:, min(k, 1), :], start=True, stop=False)
                mm(bank, q, keys, start=False, stop=True).then_inc(sa_done, 1)

            def scores(b, par, j):
                J = NH * b + j
                g, c = divmod(j, HG)
                if j in (0, NH // 2):
                    pe.wait_ge(qT_ready, 2 * b + 1 + j // (NH // 2))
                wait(pe, exp_done, J - 1)
                bank = ps_s[j % 2]
                mm(bank[:, 0:T], k_diag[par][:, g, c, P:T], qT[par][:, g, :])
                mm(bank[:, T:2 * T], k_diag[par][:, g, c, 0:P], qT[par][:, g, :])\
                    .then_inc(s_done, 1)

            def values(b, par, j):
                J = NH * b + j
                g, c = divmod(j, HG)
                if j == 0:
                    pe.wait_ge(vaug_ready, b + 1)
                pe.wait_ge(sel_done, J + 1)
                if c == 0:
                    wait(pe, oT_ready, G * b + g)
                pr = probs[j % NPB]
                q = slice(32 * c, 32 * c + 32)
                mm(ps_o[q, 0:T], v_aug[par][:, 0, j, :], pr[:, P:3 * P], start=True, stop=False,
                   tile_position=(0, 32 * c))
                mm(ps_o[q, P:T], v_aug[par][:, 1, j, :], pr[:, 0:P], start=False, stop=True,
                   tile_position=(0, 32 * c)).then_inc(pv_done, 1)

            def o_T(b, t):
                if t == 0:
                    pe.wait_ge(oT_ready, G * b + G)
                    wait(pe, lg_ready, b - 2 + CREDIT)
                else:
                    pe.wait_ge(norm_step, 4 * b + 2)
                for g in range(G):
                    last = tr(ps_b[:, g * P:(g + 1) * P], oT[:, g, t * P:(t + 1) * P], eye_f[:])
                last.then_inc(otok_psum, 1)

            def otok_T(b):
                pe.wait_ge(norm_step, 4 * b + 4)
                for t in range(TT):
                    last = tr(ps_b[:, t * P:(t + 1) * P],
                              o_tok[:, t].rearrange("p h d -> p (h d)"), eye_f[:])
                last.then_inc(otokT_done, 1)

            def project(b):
                pe.wait_ge(otokT_ready, b + 1)
                for t in range(TT):
                    last = mm(ps_b[:, t * P:(t + 1) * P], o_tokT[:, t * P:(t + 1) * P],
                              w_sb[:, 3 * D:4 * D])
                last.then_inc(y_done, 1)

            def xn2_T(b):
                pe.wait_ge(xn2_ready, b + 1)
                pe.wait_ge(at_ready, min(b + 3, B) if isinstance(b, int) else b + 3)
                for t in range(TT):
                    last = tr(ps_b[:, t * P:(t + 1) * P], xn2[:, t], eye_f[:])
                last.then_inc(xn2t_done, 1)

            def route(b):
                pe.wait_ge(xn2T_ready, b + 1)
                for t in range(TT):
                    last = mm(ps_b[:, t * NE:(t + 1) * NE], xn2T_now[:, t * P:(t + 1) * P], rw_sb[:])
                last.then_inc(lg_psum, 1)

            def hidden(i):
                for m in range(HC):
                    wait(pe, hid_ready, i * HC + m - HC + 1)
                    mm(h_bank[m], ow1_sb[:, m * P:(m + 1) * P], xn2T[:, bass.ds(i * QUAD * P, QUAD * P)])\
                        .then_inc(h_done, 1)

            def over(i, par):
                pe.wait_ge(hid_ready, i * HC + HC)
                if not isinstance(i, int) or i >= 2:
                    pe.wait_ge(over_step, (i - 2) * OVER + 1 + CREDIT)
                for c in range(QUAD):
                    for m in range(HC):
                        last = mm(y_bank[par][:, c * D:(c + 1) * D], hid[par][:, m, c * P:(c + 1) * P],
                                  ow2_sb[:, m, :], start=(m == 0), stop=(m == HC - 1))
                last.then_inc(yov_done, 1)

            def step(n, par, has):
                f1, f2, b2, b4 = has(n + 2), has(n + 1), has(n - 1), has(n - 3)
                for j in range(NH):
                    if has(n):
                        scores(n, par, j)
                    if b2 and j == 3:
                        o_T(n - 1, 0)
                    if b2 and j == 7:
                        otok_T(n - 1)
                    if f2 and j == 7:
                        max_scores(n + 1, 1 - par, 7)
                    if f2 and j == 11:
                        max_scores(n + 1, 1 - par, 10)
                    if f2 and j == 12:
                        max_scores(n + 1, 1 - par, 11)
                    if b4 and j == 12:
                        xn2_T(n - 3)
                    if f1 and j == 13:
                        k_T(n + 2, par, 0)
                    if j >= LAG and has(n):
                        values(n, par, j - LAG)
                    if j < LAG and b2:
                        values(n - 1, 1 - par, NH - LAG + j)
                    if f2 and j == 0:
                        max_scores(n + 1, 1 - par, 0)
                    if f2 and j == 1:
                        k_T(n + 1, 1 - par, 1)
                        max_scores(n + 1, 1 - par, 1)
                    if f1 and j == 1:
                        xn_T(n + 2)
                    if f2 and j == 2:
                        max_scores(n + 1, 1 - par, 2)
                    if f2 and j == 3:
                        max_scores(n + 1, 1 - par, 3)
                    if f2 and j == 4:
                        q_T(n + 1, 1 - par, 1, False)
                        max_scores(n + 1, 1 - par, 4)
                    if b2 and j == 4:
                        o_T(n - 1, 1)
                    if f1 and j == 4:
                        qkv(n + 2, 0)
                    if f2 and j == 5:
                        max_scores(n + 1, 1 - par, 5)
                    if f1 and j == 5:
                        qkv(n + 2, 1)
                    if f2 and j == 6:
                        max_scores(n + 1, 1 - par, 6)
                    if f2 and j == 8:
                        max_scores(n + 1, 1 - par, 8)
                    if f2 and j == 9:
                        max_scores(n + 1, 1 - par, 9)
                    if f2 and j == 10:
                        q_T(n + 1, 1 - par, 0, True)
                    if b2 and j == 10:
                        project(n - 1)
                    if b4 and j == 14:
                        route(n - 3)
                    if f1 and j == 15:
                        q_T(n + 2, par, 0, False)
                if f2:
                    q_T(n + 1, 1 - par, 1, True)
                for i in range(2):
                    if has(n - 1 - i) and not has(n - i):
                        pe.wait_ge(late_in, 16 * 9)
                        pe.wait_ge(xn2T_kept, QUAD // TT * (i + 1) + CREDIT)
                        pe.wait_ge(qT_ready, 2 * B)
                        pe.wait_ge(max_done, 12 * B)
                        hidden(i)

            pe.wait_ge(consts_ready, 1)
            pe.sem_inc(yov_done, 2)
            pe.sem_inc(xn2t_done, CREDIT)
            steady(pe, step)

            pe.wait_ge(exp_done, NH * B)
            over(0, 0)
            pe.wait_ge(route_step, 9)
            one_hot = hot_b[:].rearrange("p n e -> p (n e)")
            mm(ps_o[:], tri_b[:], one_hot)
            mm(ps_b[:], ones_b[:], one_hot).then_inc(rank_psum, 1)
            over(1, 1)
            pe.wait_ge(xn2T_kept, B + CREDIT)
            hidden(2)
            with pe.Fori(0, (STEPS2 - 4) // 2) as k2:
                for c in (3, 4):
                    hidden(k2 * 2 + c)
                    over(k2 * 2 + (c - 1), (c - 1) % 2)
            hidden(STEPS2 - 1)
            for i in (STEPS2 - 2, STEPS2 - 1):
                over(i, i % 2)

            pe.wait_ge(hid_ready, HC * STEPS2)
            pe.wait_ge(route_step, ROUTE)

            def tokens_T(lot):
                pe.wait_ge(xgn_ready, (lot + 1) * QUAD)
                for c in range(QUAD):
                    last = tr(g_bank[lot][:, c * HALF:(c + 1) * HALF], xgn[:, lot * QUAD + c],
                              eye_f[0:HALF, 0:HALF])
                last.then_inc(gT_psum, 1)

            pe.sem_inc(ye_done, 2)

            def expert_hidden(e):
                pe.wait_ge(w1_in[e % NW], e // NW * 16 + 16)
                for m in range(HC):
                    pe.wait_ge(hid_e_ready, e * HC + m - HC + 1 + HC)
                    mm(h_bank[m][:, 0:CAP], w1_sb[e % NW][:, m * P:(m + 1) * P],
                       xgT[:, e * CAP:(e + 1) * CAP]).then_inc(he_done, 1)

            def expert_out(e):
                pe.wait_ge(hid_e_ready, e * HC + HC + HC)
                if e < 2:
                    pe.wait_ge(w2_in, 16)
                    pe.wait_ge(last_step, e + 1)
                pe.wait_ge(ye_read, e * YE - 2 * YE + 1 + 2 * YE)
                for t in range(2):
                    for m in range(HC):
                        last = mm(y_bank[e % 2][0:HALF, t * D:(t + 1) * D],
                                  hid_e[e % 2][:, m, t * HALF:(t + 1) * HALF], w2_sb[:, e, m, :],
                                  start=(m == 0), stop=(m == HC - 1))
                last.then_inc(ye_done, 1)

            for half in range(2):
                for lot in (2 * half, 2 * half + 1):
                    tokens_T(lot)
                pe.wait_ge(xgT_ready, 2 * half + 2)
                for e in range(half * NE // 2, (half + 1) * NE // 2):
                    expert_hidden(e)
                    if e % (NE // 2):
                        expert_out(e - 1)
                expert_out(e)


def steady(eng, step):
    def edge(n):
        step(n, n % 2, lambda b: 0 <= b < B)

    for n in range(-3, 3):
        edge(n)
    with eng.Fori(0, (B - 6) // 2) as i:
        for k in (3, 4):
            step(i * 2 + k, k % 2, lambda b: True)
    for n in range(B - 3, B + 3):
        edge(n)


_INS = ("x", "w_qkvo", "bo", "cos", "sin", "masks", "eye", "router_w", "router_b", "w1", "b1", "w2",
        "b2", "ow1", "ob1", "ow2", "ob2", "tri", "rank_table", "tokens", "idx_init")


def shape_tables(np):
    inv = (1.0 / (np.float32(10000.0) ** (np.arange(0, DH, 2, dtype=np.float32) / np.float32(DH)))).astype(np.float32)
    ang = np.arange(T, dtype=np.float32)[:, None] * inv[None, :]
    ang = np.concatenate([ang, ang], -1)
    tile = lambda a: np.ascontiguousarray(a.reshape(TT, P, DH).transpose(1, 0, 2), dtype=np.float32)
    sin = np.sin(ang)
    sin[:, :DH // 2] *= -1.0
    q, k = np.arange(P)[:, None], np.arange(P)[None, :]
    causal = np.where(k <= q, 0.0, NEG)
    window = np.concatenate([np.where(k > q, 0.0, NEG), causal], 1)
    masks = np.stack([np.tile(causal, (1, HG)), np.tile(window, (1, 2))], 1).astype(np.float32)
    return {"cos": tile(np.cos(ang)), "sin": tile(sin), "masks": masks,
            "eye": np.eye(P, dtype=np.float32),
            "rank_table": np.ascontiguousarray(np.broadcast_to(
                np.stack([NE - np.arange(NE), CAP * np.arange(NE) - 1.0])[None], (P, 2, NE)), dtype=np.float32),
            "tokens": np.ascontiguousarray(np.arange(N, dtype=np.int32).reshape(NT, P).T),
            "tri": (q <= k).astype(np.float32),
            "idx_init": np.full((SLOTS, 1), LAST, np.int32)}


def kernel(**inputs):
    import numpy as np
    import concourse.bacc as bacc
    from concourse.bass_utils import run_bass_kernel_spmd

    a = {k.replace("L0_attn_", "").replace("L0_ffn_", ""): np.asarray(v) for k, v in inputs.items()}
    rows = lambda v, n=P: np.ascontiguousarray(np.broadcast_to(v[None], (n, *v.shape)))
    data = shape_tables(np)
    data["x"] = np.ascontiguousarray(a["query"].reshape(N, D))
    data["w_qkvo"] = np.ascontiguousarray(np.concatenate([a[w].T for w in ("Wq", "Wk", "Wv", "Wo")], 1))
    data["bo"] = rows(a["bo"])
    data["router_w"] = a["router_w"]
    data["router_b"] = rows(a["router_b"])
    data["w1"] = a["w1"]
    data["b1"] = np.ascontiguousarray(a["b1"].reshape(NE, HC, P).transpose(2, 0, 1))
    data["w2"] = a["w2"]
    data["b2"] = rows(a["b2"])
    data["ow1"] = a["ow1"]
    data["ob1"] = np.ascontiguousarray(a["ob1"].reshape(HC, P).T)
    data["ow2"] = a["ow2"]
    data["ob2"] = rows(a["ob2"])

    nc = bacc.Bacc("TRN2", target_bir_lowering=False, num_devices=1)
    dram, args = {}, []
    for name in _INS:
        arr = np.ascontiguousarray(data[name])
        dram[f"in_{name}"] = arr
        args.append(nc.dram_tensor(f"in_{name}", arr.shape, mybir.dt.from_np(arr.dtype), kind="ExternalInput").ap())
    out = nc.dram_tensor("out_x", (N, D), F32, kind="ExternalOutput").ap()
    slot_tok = nc.dram_tensor("slot_tok", (SLOTS, 1), I32, kind="Internal").ap()
    x1_dram = nc.dram_tensor("x1_dram", (N, D), F32, kind="Internal").ap()
    layer_kernel(nc, *args, out, slot_tok, x1_dram)
    r = run_bass_kernel_spmd(nc, [dram], core_ids=[0])
    return np.asarray(r.results[0]["out_x"]).reshape(B, T, D)
```
